# Optimizing a Trainium2 kernel written in Bass

```python
import numpy as np
import jax
import jax.numpy as jnp

def _softmax(x, axis=-1):
    return jax.nn.softmax(x, axis=axis)

def _gelu(x):
    return jax.nn.gelu(x, approximate=True)

def _silu(x):
    return jax.nn.silu(x)

def _sigmoid(x):
    return jax.nn.sigmoid(x)

def _layernorm(x, axis=-1, eps=1e-05):
    m = jnp.mean(x, axis=axis, keepdims=True)
    v = jnp.var(x, axis=axis, keepdims=True)
    return (x - m) / jnp.sqrt(v + eps)

def _scatter_add(tgt, idx, src, axis=0):
    return tgt.at[idx].add(src)

def _segment_sum(src, seg, n):
    return jax.ops.segment_sum(src, seg, n)
kernel_name = 'mk_gnn_resnorm_d2_gnn_r8_6c278c'

def setup_inputs(seed: int=0):
    np.random.seed(seed)
    _w = jnp.asarray

    def _rec_inputs():
        import jax
        import jax.numpy as jnp
        _gk = jax.random.key(seed)
        x = -0.0002117 + 1 * jax.random.normal(jax.random.fold_in(_gk, 1), (6250, 512), jnp.float32)
        _s = jax.random.randint(jax.random.fold_in(_gk, 2), (50000,), 0, 6250, jnp.int32)
        _d = jax.random.randint(jax.random.fold_in(_gk, 3), (50000,), 0, 6250, jnp.int32)
        _loop = jnp.arange(6250, dtype=jnp.int32)
        src = jnp.concatenate([_s, _d, _loop])
        dst = jnp.concatenate([_d, _s, _loop])
        _o = jnp.argsort(dst, stable=True)
        src = src[_o]
        dst = dst[_o]
        return (x, src, dst)
    x, src, dst = _rec_inputs()

    def _L0_gnn_setup():
        import jax, jax.numpy as jnp
        import numpy as np
        N_NODES = 6250
        N_EDGES = 50000
        D = 512
        SELF_LOOP_W = 2.0

        def _gcn_layer(x, W, b, src, dst, n_nodes):
            h = x @ W
            ones = jnp.ones(src.shape[0], dtype=h.dtype)
            deg = jax.ops.segment_sum(ones, dst, num_segments=n_nodes) + SELF_LOOP_W
            dinv = jnp.where(deg > 0, jax.lax.rsqrt(deg), 0.0)
            norm = dinv[src] * dinv[dst]
            msgs = h[src] * norm[:, None]
            agg = jax.ops.segment_sum(msgs, dst, num_segments=n_nodes)
            agg = agg + h * (SELF_LOOP_W * dinv * dinv)[:, None]
            return agg + b
        key = jax.random.key(seed)
        k0, k1, k2, k3 = jax.random.split(key, 4)
        t_rep = jax.random.normal(k0, (N_NODES, D), dtype=jnp.float32)
        edge_index = jax.random.randint(k1, (2, N_EDGES), 0, N_NODES, dtype=jnp.int64)
        W1 = jax.random.normal(k2, (D, D), dtype=jnp.float32) / np.sqrt(D).astype(np.float32)
        b1 = jnp.zeros((D,), jnp.float32)
        W2 = jax.random.normal(k3, (D, D), dtype=jnp.float32) / np.sqrt(D).astype(np.float32)
        b2 = jnp.zeros((D,), jnp.float32)
        return {'t_rep': t_rep, 'edge_index': edge_index, 'W1': W1, 'b1': b1, 'W2': W2, 'b2': b2}
    _L0_gnn_all = _L0_gnn_setup()
    _L0_gnn_in = {k: v for k, v in _L0_gnn_all.items() if k in ('W1', 'b1', 'W2', 'b2')}
    del _L0_gnn_all

    def _L1_gnn_setup():
        import jax, jax.numpy as jnp
        import numpy as np
        N_NODES = 6250
        key = jax.random.key(seed)
        ks = jax.random.split(key, 5)
        d_in, d_out = (512, 512)
        n_edges = 100000
        x = jax.random.normal(ks[0], (N_NODES, d_in), dtype=jnp.float32)
        edge_index = jax.random.randint(ks[1], (2, n_edges), 0, N_NODES, dtype=jnp.int64)
        s = 1.0 / np.sqrt(d_in)
        W_l = jax.random.uniform(ks[2], (d_out, d_in), dtype=jnp.float32, minval=-s, maxval=s)
        b_l = jax.random.uniform(ks[3], (d_out,), dtype=jnp.float32, minval=-s, maxval=s)
        W_r = jax.random.uniform(ks[4], (d_out, d_in), dtype=jnp.float32, minval=-s, maxval=s)
        return {'x': x, 'edge_index': edge_index, 'W_l': W_l, 'b_l': b_l, 'W_r': W_r}
    _L1_gnn_all = _L1_gnn_setup()
    _L1_gnn_in = {k: v for k, v in _L1_gnn_all.items() if k in ('W_l', 'b_l', 'W_r')}
    del _L1_gnn_all
    return {'x': x, 'src': src, 'dst': dst, 'L0_gnn_W1': _L0_gnn_in['W1'], 'L0_gnn_b1': _L0_gnn_in['b1'], 'L0_gnn_W2': _L0_gnn_in['W2'], 'L0_gnn_b2': _L0_gnn_in['b2'], 'L1_gnn_W_l': _L1_gnn_in['W_l'], 'L1_gnn_b_l': _L1_gnn_in['b_l'], 'L1_gnn_W_r': _L1_gnn_in['W_r']}

def reference(x, src, dst, L0_gnn_W1, L0_gnn_b1, L0_gnn_W2, L0_gnn_b2, L1_gnn_W_l, L1_gnn_b_l, L1_gnn_W_r):
    import jax
    import jax.numpy as jnp

    def _L0_gnn_ref(t_rep, edge_index, W1, b1, W2, b2):
        import jax, jax.numpy as jnp
        import numpy as np
        N_NODES = 6250
        N_EDGES = 50000
        D = 512
        SELF_LOOP_W = 2.0

        def _gcn_layer(x, W, b, src, dst, n_nodes):
            h = x @ W
            ones = jnp.ones(src.shape[0], dtype=h.dtype)
            deg = jax.ops.segment_sum(ones, dst, num_segments=n_nodes) + SELF_LOOP_W
            dinv = jnp.where(deg > 0, jax.lax.rsqrt(deg), 0.0)
            norm = dinv[src] * dinv[dst]
            msgs = h[src] * norm[:, None]
            agg = jax.ops.segment_sum(msgs, dst, num_segments=n_nodes)
            agg = agg + h * (SELF_LOOP_W * dinv * dinv)[:, None]
            return agg + b
        src, dst = (edge_index[0], edge_index[1])
        x = _gcn_layer(t_rep, W1, b1, src, dst, N_NODES)
        x = jax.nn.relu(x)
        x = _gcn_layer(x, W2, b2, src, dst, N_NODES)
        x = jax.nn.relu(x)
        return x

    def _L1_gnn_ref(x, edge_index, W_l, b_l, W_r):
        import jax, jax.numpy as jnp
        import numpy as np
        N_NODES = 6250
        x_l = x @ W_l.T + b_l
        src, dst = (edge_index[0], edge_index[1])
        agg = jax.ops.segment_sum(x_l[src], dst, num_segments=N_NODES)
        deg = jax.ops.segment_sum(jnp.ones_like(src, dtype=x.dtype), dst, num_segments=N_NODES)
        out_l = agg / jnp.maximum(deg, 1.0)[:, None]
        out_r = x @ W_r.T
        return out_l + out_r
    edge_index = jnp.stack([src, dst])
    x = _layernorm(x + _L0_gnn_ref(x, edge_index, L0_gnn_W1, L0_gnn_b1, L0_gnn_W2, L0_gnn_b2), axis=-1)
    x = _layernorm(x + _L1_gnn_ref(x, edge_index, L1_gnn_W_l, L1_gnn_b_l, L1_gnn_W_r), axis=-1)
    return x

_drawn_inputs = setup_inputs


def setup_inputs(seed=0):
    import zlib

    import numpy as np

    out = dict(_drawn_inputs(seed))
    spreads = {'L0_gnn_b1': (0.0, 0.1), 'L0_gnn_b2': (0.0, 0.1)}
    factors = {'L1_gnn_b_l': 2.739}
    for name, (base, spread) in spreads.items():
        noise = np.random.default_rng([zlib.crc32(name.encode()), seed]).standard_normal(out[name].shape)
        drawn = base * np.exp(spread * noise) if base else spread * noise
        out[name] = jnp.asarray(drawn.astype(out[name].dtype))
    for name, factor in factors.items():
        out[name] = (out[name] * factor).astype(out[name].dtype)
    return out
```

```python
from contextlib import ExitStack

import concourse.bass as bass
from concourse import mybir

P = 128
D = 512
KD = D // P
CHUNKS = 4
GROUP = CHUNKS * P
SLOTS = 4
BODY = SLOTS * CHUNKS
SPLIT = 2
EPS = 1e-5
SELF_LOOP_W = 2.0


def gnn_program(nc, n_nodes, x, src, dst, dst_groups, w1, b1, w2, b2, wl, bl, wr, out):
    fp32 = mybir.dt.float32
    fp32r = mybir.dt.float32r
    bf16 = mybir.dt.bfloat16
    i32 = mybir.dt.int32
    ALU = mybir.AluOpType
    ACT = mybir.ActivationFunctionType
    AX = mybir.AxisListType

    TILES = -(-n_nodes // P)
    ROWS = TILES * P
    GROUPS = dst_groups.shape[0]
    BODIES = GROUPS // SLOTS
    COLS = GROUPS * CHUNKS
    HALVES = -(-GROUPS // P)
    GROWS = GROUPS // HALVES
    LAST = TILES - 1
    assert GROWS * HALVES == GROUPS and BODIES * SLOTS == GROUPS and TILES >= 6

    table = [nc.dram_tensor(f"table{n}", (ROWS, D), fp32, kind="Internal").ap() for n in range(3)]
    raw_dram = nc.dram_tensor("raw_ranges", (2, GROUPS), i32, kind="Internal").ap()
    range_dram = nc.dram_tensor("ranges_dram", (1, 2 * GROUPS + 1), i32, kind="Internal").ap()

    ctx = ExitStack()
    with ctx:
        def sb(name, shape, dt):
            return ctx.enter_context(nc.sbuf_tensor(name, shape, dt))

        def pb(name, shape, dt=fp32):
            return ctx.enter_context(nc.psum_tensor(name, shape, dt))

        def sem(name):
            return ctx.enter_context(nc.semaphore(name))

        own = sb("own", [P, TILES, D], fp32)
        rows = sb("rows", [P, SLOTS, CHUNKS * D], fp32)
        part_hi = sb("part_hi", [P, SPLIT, CHUNKS * D], fp32r)
        part_lo = sb("part_lo", [P, SPLIT, CHUNKS * D], fp32r)
        onehot = sb("onehot", [P, SPLIT, CHUNKS, 2 * P], fp32r)
        weight_a = sb("weight_a", [P, KD, D], fp32)
        weight_b = sb("weight_b", [P, KD, D], fp32)
        bias = sb("bias", [P, D], fp32)
        agg_sb = sb("agg_sb", [P, D], fp32)
        aggT = sb("aggT", [P, D], fp32)
        pair = sb("pair", [P, 2, D], fp32)
        z = sb("z", [P, 2, D], fp32)
        dst_rel = sb("dst_rel", [P, COLS], fp32)
        src_slot = sb("src_slot", [P, SLOTS, CHUNKS], i32)
        window = sb("window", [P, 2 * P], bf16)
        ident = sb("ident", [P, P], fp32)
        twice = sb("twice", [P, P], fp32)
        zeros = sb("zeros", [P, P], bf16)
        span = sb("span", [P, 1], fp32)
        degree = sb("degree", [P, TILES], fp32)
        dinv = sb("dinv", [P, TILES], fp32)
        rmean = sb("rmean", [P, TILES], fp32)
        share = sb("share", [P, TILES], fp32)
        stats = sb("stats", [P, 6], fp32)
        moment = sb("moment", [P, 2], fp32)
        moments = sb("moments", [P, 2, 2], fp32)
        std = sb("std", [P, 2], fp32)
        rstd = sb("rstd", [P, 1], fp32)
        eps = sb("eps", [P, 1], fp32)
        ranges = sb("ranges", [1, 2 * GROUPS + 2], i32)

        rows_flat = rows[:, :, :].rearrange("p s f -> p (s f)")
        at = [0]

        def early(width, dt, size=4):
            a = at[0]
            at[0] = a + -(-width * size // 4)
            v = rows_flat[:, a:at[0]]
            return v if dt == fp32 else v.bitcast(dt)

        dst_g = early(HALVES * GROUP, i32).rearrange("p (a e) -> p a e", a=HALVES)
        dst_c = early(COLS, i32)
        dst_bits = early(COLS, i32)
        node_in_tile = early(COLS, fp32)
        tile_of = early(COLS, fp32)
        node_hot = [early(BODY * P, bf16, 2).rearrange("p (c n) -> p c n", c=BODY) for _ in range(2)]
        tile_hot = [early(BODY * TILES, bf16, 2).rearrange("p (c n) -> p c n", c=BODY) for _ in range(2)]
        assert at[0] <= SLOTS * CHUNKS * D
        z_flat = z[:, :, :].rearrange("p a f -> p (a f)")
        raw_i = z_flat[0:1, 0:2 * GROUPS].bitcast(i32)
        raw_f = z_flat[0:1, 2 * GROUPS:4 * GROUPS]
        assert 4 * GROUPS + 8 <= 2 * D
        group_range = pair[:, 0, 0:2 * HALVES].bitcast(i32).rearrange("p (m a) -> p m a", m=2)
        range_i = pair[:, 1, 0:2 * HALVES].bitcast(i32).rearrange("p (m a) -> p m a", m=2)
        masked_f = agg_sb[0:1, 0:2 * GROUPS + 1] if 2 * GROUPS + 1 <= D else None
        masked_i = aggT[0:1, 0:2 * GROUPS + 1].bitcast(i32)
        steps_f = bias[0:1, 0:GROUPS]
        steps_g = bias[0:1, GROUPS:2 * GROUPS]
        worst = std[0:1, 0:1]
        worst2 = std[0:1, 1:2]
        keep = rstd[0:1, 0:1]
        lo_all = agg_sb[:, 0:GROUPS + 1]
        lo_raw = aggT[:, 0:GROUPS + 1].bitcast(i32)

        agg_ps = pb("agg_ps", [P, 2, D])
        turn_ps = pb("turn_ps", [P, D])
        turn2_ps = pb("turn2_ps", [P, D])
        prod_ps = pb("prod_ps", [P, 2, D])
        count_ps = pb("count_ps", [P, TILES])

        consts_made = sem("consts_made")
        edges_loaded = sem("edges_loaded")
        group_rows_loaded = sem("group_rows_loaded")
        raw_stored = sem("raw_stored")
        raw_loaded = sem("raw_loaded")
        raw_made = sem("raw_made")
        masked_made = sem("masked_made")
        masked_stored = sem("masked_stored")
        ranges_loaded = sem("ranges_loaded")
        lo_loaded = sem("lo_loaded")
        dve_chain = sem("dve_chain")
        passed = sem("passed")
        digits_made = sem("digits_made")
        node_hot_made = sem("node_hot_made")
        tile_hot_made = sem("tile_hot_made")
        hots_counted = sem("hots_counted")
        counted = sem("counted")
        degree_made = sem("degree_made")
        root_made = sem("root_made")
        x_own_loaded = [sem(f"x_own_loaded{n}") for n in range(7)]
        scaled = sem("scaled")
        weights_loaded = [sem(f"weights_loaded{n}") for n in range(3)]
        bias_loaded = [sem(f"bias_loaded{n}") for n in range(3)]
        table_stored = [sem(f"table_stored{n}") for n in range(4)]
        layer_read = sem("layer_read")
        src_loaded = [sem(f"src_loaded{s}") for s in range(SLOTS)]
        gathered = [sem(f"gathered{s}") for s in range(SLOTS)]
        hi_made = sem("hi_made")
        lo_made = sem("lo_made")
        onehot_made = sem("onehot_made")
        split_free = sem("split_free")
        agg_done = [sem(f"agg_done{n}") for n in range(3)]
        agg_taken = [sem(f"agg_taken{n}") for n in range(3)]
        own_taken = sem("own_taken")
        turned = [sem(f"turned{n}") for n in range(3)]
        aggT_made = [sem(f"aggT_made{n}") for n in range(3)]
        prod_done = [sem(f"prod_done{n}") for n in range(3)]
        prod_free = [sem(f"prod_free{n}") for n in range(3)]
        pair_loaded = sem("pair_loaded")
        pair_free = sem("pair_free")
        stats_made = [sem(f"stats_made{n}") for n in range(3)]
        std_made = [sem(f"std_made{n}") for n in range(3)]
        own_made = [sem(f"own_made{n}") for n in range(3)]

        tiles = []
        scale_of = [dinv, dinv, rmean]
        stored_to = [table[1], table[2], out]

        def passes_of(eng):
            return eng.value_load(ranges[0:1, 2 * GROUPS:2 * GROUPS + 1], min_val=1, max_val=TILES)

        def stand_alone(eng):
            eng.sem_inc(passed, 1)

        def as_tile(eng, value):
            tile = eng.alloc_register(f"tile{len(tiles)}")
            tiles.append(tile)
            eng.reg_mov(tile, value)
            return eng.snap(tile, min_val=0, max_val=LAST)

        def lo_of(eng, g, r):
            return as_tile(eng, eng.value_load(ranges[0:1, bass.ds(g, 1)], min_val=0, max_val=LAST) + r)

        def hi_of(eng, g, r):
            return as_tile(eng, eng.value_load(ranges[0:1, bass.ds(GROUPS + g, 1)], min_val=0, max_val=LAST) + r)

        def back(eng, t, k):
            if isinstance(t, int):
                return t - k
            tile = eng.alloc_register(f"tile{len(tiles)}")
            tiles.append(tile)
            eng.reg_alu(tile, eng.snap(t - k), 0, ALU.max)
            return eng.snap(tile, min_val=0, max_val=LAST)

        def tile_cols(n):
            a = -(-TILES // 7)
            return min(n * a, TILES), min((n + 1) * a, TILES)

        block = ctx.enter_context(nc.Block())

        @block.sync
        def _(sp):
            sp.dma_start(dst_g[0:GROWS], dst_groups.rearrange("(a p) e -> p a e", p=GROWS)).then_inc(group_rows_loaded, 16)
            sp.dma_start(dst_c, dst).then_inc(edges_loaded, 16)
            for n in range(7):
                a, b = tile_cols(n)
                if a < b:
                    sp.dma_start(own[:, a:b, :], x[a * P:b * P, :].rearrange("(t p) f -> p t f", p=P))\
                      .then_inc(x_own_loaded[n], 16)
            for s in range(SLOTS):
                sp.dma_start(src_slot[:, s, :], src[:, s * CHUNKS:(s + 1) * CHUNKS]).then_inc(src_loaded[s], 16)
            sp.wait_ge(raw_made, 1)
            sp.dma_start(raw_dram.rearrange("m (a p) -> p m a", p=GROWS), range_i[0:GROWS],
                         allow_slow_non_contiguous=True).then_inc(raw_stored, 16)
            sp.wait_ge(raw_stored, 16)
            sp.dma_start(raw_i, raw_dram.rearrange("m (o g) -> o (m g)", o=1)).then_inc(raw_loaded, 16)
            sp.wait_ge(masked_made, 1)
            sp.dma_start(range_dram, masked_i).then_inc(masked_stored, 16)
            sp.wait_ge(masked_stored, 16)
            sp.dma_start(ranges[0:1, 0:2 * GROUPS + 1], range_dram).then_inc(ranges_loaded, 16)
            sp.dma_start(lo_raw[:, 0:GROUPS], range_dram[0:1, 0:GROUPS].to_broadcast([P, GROUPS]))\
              .then_inc(lo_loaded, 16)
            sp.dma_start(lo_raw[:, GROUPS:GROUPS + 1], range_dram[0:1, 2 * GROUPS:2 * GROUPS + 1].to_broadcast([P, 1]))\
              .then_inc(lo_loaded, 16)
            sp.dma_start(weight_a[:, :, :], w1.rearrange("(k p) n -> p k n", p=P)).then_inc(weights_loaded[0], 16)
            sp.dma_start(weight_b[:, :, :], w2.rearrange("(k p) n -> p k n", p=P)).then_inc(weights_loaded[1], 16)
            sp.wait_ge(ranges_loaded, 16)
            passes = passes_of(sp)
            for layer, b in enumerate((b1, b2, bl)):
                sp.wait_ge(layer_read, layer + 1)
                sp.dma_start(bias[:, :], b.to_broadcast([P, D])).then_inc(bias_loaded[layer], 16)
                if layer == 1:
                    sp.dma_start(weight_a[:, :, :], wl.rearrange("(k p) n -> p k n", p=P))\
                      .then_inc(weights_loaded[2], 16)
                if layer == 2:
                    sp.dma_start(weight_b[:, :, :], wr.rearrange("(k p) n -> p k n", p=P))\
                      .then_inc(weights_loaded[2], 16)
                base = sp.snap(passes * (layer * BODIES))
                with sp.Fori(0, passes) as r:
                    with sp.Fori(0, BODIES) as i:
                        n = sp.snap(base + r * BODIES + i + 1)
                        for s in range(SLOTS):
                            sp.wait_ge(gathered[s], n * (16 * CHUNKS))
                            sp.dma_start(src_slot[:, s, :], src[:, bass.ds(i * BODY + BODY + s * CHUNKS, CHUNKS)])\
                              .then_inc(src_loaded[s], 16)
            for s in range(SLOTS):
                sp.wait_ge(src_loaded[s], sp.snap(passes * (3 * BODIES * 16) + 16))
            stand_alone(sp)

        @block.gpsimd
        def _(pool):
            pool.iota(window[:, :], pattern=[[1, 2 * P]], base=0, channel_multiplier=0,
                      allow_small_or_imprecise_dtypes=True).then_inc(consts_made, 1)
            pool.memset(zeros[:, :], 0.0).then_inc(consts_made, 1)
            pool.memset(eps[:, :], EPS).then_inc(consts_made, 1)
            pool.memset(ident[:, :], 0.0).then_inc(consts_made, 1)
            pool.memset(twice[:, :], 0.0).then_inc(consts_made, 1)
            pool.wait_ge(consts_made, 5)
            for m, v in ((ident, 1.0), (twice, SELF_LOOP_W)):
                pool.affine_select(out=m[:, :], in_=m[:, :], compare_op=ALU.not_equal, fill=v, base=0,
                                   pattern=[[-1, P]], channel_multiplier=1).then_inc(consts_made, 1)
            pool.wait_ge(ranges_loaded, 16)
            passes = passes_of(pool)
            for layer in range(3):
                pool.wait_ge(table_stored[layer], 16 * (7 if layer == 0 else TILES))
                base = pool.snap(passes * (layer * BODIES))
                with pool.Fori(0, passes) as r:
                    with pool.Fori(0, BODIES) as i:
                        n = pool.snap(base + r * BODIES + i)
                        for s in range(SLOTS):
                            pool.wait_ge(src_loaded[s], n * 16 + 16)
                            pool.wait_ge(lo_made, n * SLOTS + (s + 1))
                            stand_alone(pool)
                            for c in range(CHUNKS):
                                pool.indirect_dma_start(
                                    rows[:, s, c * D:(c + 1) * D], None, table[layer],
                                    bass.IndirectOffsetOnAxis(ap=src_slot[:, s, c:c + 1], axis=0))\
                                    .then_inc(gathered[s], 16)

        @block.scalar
        def _(act):
            act.wait_ge(consts_made, 7)
            act.wait_ge(degree_made, 1)
            act.activation(degree[:, :], degree[:, :], ACT.Sqrt).then_inc(root_made, 1)
            for n in range(7):
                a, b = tile_cols(n)
                act.wait_ge(scaled, n + 1)
                if a < b:
                    act.dma_start(table[0][a * P:b * P, :].rearrange("(t p) f -> p t f", p=P), own[:, a:b, :])\
                       .then_inc(table_stored[0], 16)
            act.wait_ge(ranges_loaded, 16)
            passes = passes_of(act)
            seen = act.alloc_register("act_seen")
            for layer in range(3):
                normed = layer > 0

                def take_sums(t):
                    act.wait_ge(turned[layer], t + 1)
                    if layer == 2:
                        act.activation(pair[:, 0, :], own[:, bass.ds(t, 1), :], ACT.Copy).then_inc(own_taken, 1)
                    act.wait_ge(agg_done[layer], t + 1)
                    act.activation(agg_sb[:, :], agg_ps[:, bass.ds(t % 2, 1), :], ACT.Identity,
                                   scale=scale_of[layer][:, bass.ds(t, 1)]).then_inc(agg_taken[layer], 1)

                def take_turned(k):
                    act.wait_ge(turned[layer], k + 2)
                    if layer == 2:
                        act.activation(pair[:, 1, :], turn2_ps[:, :], ACT.Copy)
                    act.activation(aggT[:, :], turn_ps[:, :], ACT.Copy).then_inc(aggT_made[layer], 1)

                def take_root(k):
                    act.wait_ge(stats_made[layer], k + 1)
                    act.activation(std[:, bass.ds(k % 2, 1)], moments[:, bass.ds(k % 2, 1), 1:2], ACT.Sqrt,
                                   bias=eps[:, 0:1]).then_inc(std_made[layer], 1)

                def load_x(k):
                    act.wait_ge(pair_free, k + 1)
                    act.dma_start(pair[:, bass.ds(k % 2, 1), :], x[bass.ds(k * P, P), :]).then_inc(pair_loaded, 16)

                def store(k):
                    act.wait_ge(own_made[layer], k + 3)
                    act.dma_start(stored_to[layer][bass.ds(k * P, P), :], own[:, bass.ds(k, 1), :])\
                       .then_inc(table_stored[layer + 1], 16)

                def step(t):
                    take_sums(t)
                    with act.If(t > 0):
                        take_turned(back(act, t, 1))
                    act.nop()
                    if layer == 1:
                        with act.If(t > 1):
                            k = back(act, t, 1)
                            act.wait_ge(pair_loaded, k * 16)
                            load_x(k)
                        act.nop()
                    if normed:
                        with act.If(t > 2):
                            take_root(back(act, t, 3))
                        act.nop()
                        with act.If(t > 4):
                            store(back(act, t, 5))
                        act.nop()
                    else:
                        with act.If(t > 2):
                            store(back(act, t, 3))
                        act.nop()

                if layer == 1:
                    act.dma_start(pair[:, 0, :], x[0:P, :]).then_inc(pair_loaded, 16)
                act.reg_mov(seen, 0)
                base = act.snap(passes * (layer * BODIES * SLOTS))
                before = act.alloc_register(f"act_before{layer}")
                act.reg_mov(before, 0)
                with act.Fori(0, passes) as r:
                    with act.Fori(0, BODIES) as i:
                        n = act.snap(base + (r * BODIES + i) * SLOTS)
                        m = act.snap((passes * (layer * BODIES) + r * BODIES + i + 1) * (16 * CHUNKS))
                        for s in range(SLOTS):
                            act.wait_ge(split_free, n + (s + 1))
                            act.wait_ge(gathered[s], m)
                            act.activation(part_hi[:, s % SPLIT, :], rows[:, s, :], ACT.Copy).then_inc(hi_made, 1)
                            done = act.snap(before, min_val=0, max_val=LAST)
                            first = act.snap(seen, min_val=0, max_val=LAST)
                            with act.If(done > first):
                                with act.Fori(first, done) as t:
                                    step(as_tile(act, t))
                                act.reg_mov(seen, done)
                            act.reg_mov(before, hi_of(act, i * SLOTS + s, r))
                first = act.snap(seen, min_val=0, max_val=LAST)
                with act.If(first < LAST):
                    with act.Fori(first, LAST) as t:
                        step(as_tile(act, t))
                act.nop()
                t = LAST
                take_sums(t)
                take_turned(back(act, t, 1))
                if layer == 1:
                    act.wait_ge(pair_loaded, 16 * (t - 1))
                    load_x(back(act, t, 1))
                    act.wait_ge(pair_loaded, 16 * t)
                    load_x(t)
                if normed:
                    take_root(back(act, t, 3))
                    store(back(act, t, 5))
                take_turned(t)
                if normed:
                    for k in range(t - 2, t + 1):
                        take_root(k)
                        store(k - 2)
                    store(back(act, t, 1))
                    store(t)
                else:
                    for k in range(t - 3, t + 1):
                        store(k)
            act.wait_ge(table_stored[3], 16 * TILES)

        @block.vector
        def _(dve):
            chain = [0]

            def link(ins):
                chain[0] += 1
                ins.then_inc(dve_chain, 1)
                dve.wait_ge(dve_chain, chain[0])

            dve.wait_ge(group_rows_loaded, 16)
            link(dve.tensor_reduce(group_range[0:GROWS, 0, :], dst_g[0:GROWS], AX.X, ALU.min))
            link(dve.tensor_reduce(group_range[0:GROWS, 1, :], dst_g[0:GROWS], AX.X, ALU.max))
            dve.tensor_scalar(range_i[0:GROWS], group_range[0:GROWS], 7, None, ALU.arith_shift_right)\
               .then_inc(raw_made, 1)
            dve.wait_ge(edges_loaded, 16)
            link(dve.tensor_scalar(dst_bits, dst_c, P - 1, None, ALU.bitwise_and))
            link(dve.tensor_copy(node_in_tile, dst_bits))
            link(dve.tensor_scalar(dst_bits, dst_c, 7, None, ALU.arith_shift_right))
            dve.tensor_copy(tile_of, dst_bits).then_inc(digits_made, 1)
            dve.tensor_copy(dst_rel[:, :], dst_c).then_inc(digits_made, 1)
            dve.wait_ge(raw_loaded, 16)
            link(dve.tensor_copy(raw_f, raw_i))
            lo_f, hi_f = raw_f[:, 0:GROUPS], raw_f[:, GROUPS:2 * GROUPS]
            link(dve.tensor_tensor(steps_f, hi_f, lo_f, ALU.subtract))
            link(dve.tensor_reduce(worst, steps_f, AX.X, ALU.max))
            link(dve.tensor_tensor(steps_g[:, 0:GROUPS - 1], hi_f[:, 0:GROUPS - 1], lo_f[:, 1:GROUPS], ALU.subtract))
            link(dve.tensor_reduce(worst2, steps_g[:, 0:GROUPS - 1], AX.X, ALU.max))
            link(dve.tensor_scalar(worst, worst, 1.0, None, ALU.subtract))
            link(dve.tensor_tensor(worst, worst, worst2, ALU.max))
            link(dve.tensor_scalar(keep, worst, 1.0, None, ALU.is_lt))
            link(dve.tensor_scalar(masked_f[:, 0:2 * GROUPS], raw_f, keep, None, ALU.mult))
            link(dve.tensor_scalar(masked_f[:, 2 * GROUPS:2 * GROUPS + 1], keep, -float(TILES - 1), float(TILES),
                                   ALU.mult, ALU.add))
            dve.tensor_copy(masked_i, masked_f).then_inc(masked_made, 1)
            dve.wait_ge(consts_made, 7)
            dve.wait_ge(digits_made, 2)
            with dve.Fori(0, BODIES // 2) as i:
                for s in range(2):
                    dve.wait_ge(hots_counted, i * 2 + (s + 1))
                    for c in range(BODY):
                        made = dve.tensor_scalar(node_hot[s][:, c, :], window[:, 0:P],
                                                 node_in_tile[:, bass.ds((i * 2 + s) * BODY + c, 1)], None, ALU.is_equal)
                    made.then_inc(node_hot_made, 1)
                    dve.tensor_tensor(
                        tile_hot[s][:, :, :],
                        window[:, 0:TILES].rearrange("p (o n) -> p o n", o=1).to_broadcast([P, BODY, TILES]),
                        tile_of[:, bass.ds((i * 2 + s) * BODY, BODY)].rearrange("p (c o) -> p c o", o=1)
                        .to_broadcast([P, BODY, TILES]),
                        ALU.is_equal).then_inc(tile_hot_made, 1)
            dve.wait_ge(counted, 1)
            link(dve.tensor_copy(rmean[:, :], count_ps[:, :]))
            dve.tensor_scalar(degree[:, :], rmean[:, :], SELF_LOOP_W, None, ALU.add).then_inc(degree_made, 1)
            link(dve.tensor_scalar(dinv[:, :], rmean[:, :], 1.0, None, ALU.max))
            link(dve.tensor_copy(share[:, :], rmean[:, :]))
            link(dve.reciprocal(rmean[:, :], dinv[:, :]))
            link(dve.tensor_tensor(share[:, :], share[:, :], rmean[:, :], ALU.mult))
            dve.wait_ge(root_made, 1)
            link(dve.reciprocal(dinv[:, :], degree[:, :]))
            for n in range(7):
                a, b = tile_cols(n)
                last = None
                if a < b:
                    dve.wait_ge(x_own_loaded[n], 16)
                for t in range(a, b):
                    last = dve.tensor_scalar(own[:, t, :], own[:, t, :], dinv[:, t:t + 1], None, ALU.mult)
                (last or dve.nop()).then_inc(scaled, 1)
            dve.wait_ge(lo_loaded, 32)
            link(dve.tensor_copy(lo_all, lo_raw))
            link(dve.tensor_scalar(lo_all, lo_all, float(P), None, ALU.mult))
            rel = dst_rel[:, :].rearrange("p (g c) -> p g c", c=CHUNKS)
            link(dve.tensor_tensor(rel, rel, lo_all[:, 0:GROUPS].rearrange("p (g o) -> p g o", o=1)
                                   .to_broadcast([P, GROUPS, CHUNKS]), ALU.subtract))
            dve.tensor_copy(span[:, :], lo_all[:, GROUPS:GROUPS + 1])
            dve.sem_inc(layer_read, 1)
            dve.wait_ge(ranges_loaded, 16)
            passes = passes_of(dve)
            seen = dve.alloc_register("dve_seen")
            links = dve.alloc_register("dve_links")
            linked = sem("linked")
            dve.reg_mov(links, 0)
            rel_moved = [0]
            for layer in range(3):
                def chained(ins):
                    ins.then_inc(linked, 1)
                    v = dve.snap(dve.snap(links) + 1)
                    dve.reg_mov(links, v)
                    dve.wait_ge(linked, v)
                    stand_alone(dve)

                def take_product(k):
                    dve.wait_ge(prod_done[layer], k + 1)
                    dve.wait_ge(own_made[layer], k + 1)
                    zk = z[:, bass.ds(k % 2, 1), :]
                    pk = prod_ps[:, bass.ds(k % 2, 1), :]
                    bk = bias[:, :].rearrange("p (o f) -> p o f", o=1)
                    if layer < 2:
                        ins = dve.tensor_tensor(zk, pk, bk, ALU.add)
                    else:
                        ins = dve.scalar_tensor_tensor(out=zk, in0=bk, scalar=share[:, bass.ds(k, 1)], in1=pk,
                                                       op0=ALU.mult, op1=ALU.add)
                    ins.then_inc(prod_free[layer], 1)
                    dve.wait_ge(prod_free[layer], k + 3)

                def finish_first(k):
                    take_product(k)
                    dve.tensor_scalar(own[:, bass.ds(k, 1), :], z[:, bass.ds(k % 2, 1), :], 0.0,
                                      dinv[:, bass.ds(k, 1)], ALU.max, ALU.mult).then_inc(own_made[layer], 1)

                def take_stats(k):
                    take_product(k)
                    zk = z[:, bass.ds(k % 2, 1), :]
                    if layer == 1:
                        dve.wait_ge(pair_loaded, k * 16 + 16)
                        ins = dve.scalar_tensor_tensor(out=zk, in0=zk, scalar=0.0, in1=pair[:, bass.ds(k % 2, 1), :],
                                                       op0=ALU.max, op1=ALU.add)
                        ins.then_inc(pair_free, 1)
                        dve.wait_ge(pair_free, k + 3)
                        stand_alone(dve)
                    else:
                        chained(dve.tensor_tensor(zk, zk, own[:, bass.ds(k, 1), :], ALU.add))
                    chained(dve.bn_stats(stats[:, :], z[:, bass.ds(k % 2, 1), :]))
                    chained(dve.bn_aggr(moment[:, :], stats[:, :]))
                    dve.tensor_copy(moments[:, bass.ds(k % 2, 1), :], moment[:, :]).then_inc(stats_made[layer], 1)

                def norm(k):
                    dve.wait_ge(std_made[layer], k + 1)
                    dve.wait_ge(own_made[layer], k + 2)
                    chained(dve.reciprocal(rstd[:, :], std[:, bass.ds(k % 2, 1)]))
                    dve.tensor_scalar(own[:, bass.ds(k, 1), :], z[:, bass.ds(k % 2, 1), :],
                                      moments[:, bass.ds(k % 2, 1), 0:1], rstd[:, 0:1],
                                      ALU.subtract, ALU.mult).then_inc(own_made[layer], 1)

                def step(t):
                    if layer == 0:
                        with dve.If(t > 1):
                            finish_first(back(dve, t, 2))
                        dve.nop()
                    else:
                        with dve.If(t > 3):
                            norm(back(dve, t, 4))
                        dve.nop()
                        with dve.If(t > 1):
                            take_stats(back(dve, t, 2))
                        dve.nop()

                dve.wait_ge(bias_loaded[layer], 16)
                dve.reg_mov(seen, 0)
                before = dve.alloc_register(f"dve_before{layer}")
                dve.reg_mov(before, 0)
                base = dve.snap(passes * (layer * BODIES * SLOTS))
                with dve.Fori(0, passes) as r:
                    with dve.Fori(0, BODIES) as i:
                        n = dve.snap(base + (r * BODIES + i) * SLOTS)
                        for s in range(SLOTS):
                            dve.wait_ge(split_free, n + (s + 1))
                            for c in range(CHUNKS):
                                made = dve.tensor_scalar(onehot[:, s % SPLIT, c, :], window[:, :],
                                                         dst_rel[:, bass.ds(i * BODY + (s * CHUNKS + c), 1)], None,
                                                         ALU.is_equal)
                            made.then_inc(onehot_made, 1)
                            dve.wait_ge(hi_made, n + (s + 1))
                            dve.tensor_tensor(part_lo[:, s % SPLIT, :], rows[:, s, :], part_hi[:, s % SPLIT, :],
                                              ALU.subtract).then_inc(lo_made, 1)
                            done = dve.snap(before, min_val=0, max_val=LAST)
                            first = dve.snap(seen, min_val=0, max_val=LAST)
                            with dve.If(done > first):
                                with dve.Fori(first, done) as t:
                                    step(as_tile(dve, t))
                                dve.reg_mov(seen, done)
                            dve.reg_mov(before, hi_of(dve, i * SLOTS + s, r))
                    dve.wait_ge(onehot_made, dve.snap(base + r * GROUPS + GROUPS))
                    chained(dve.tensor_scalar(dst_rel[:, :], dst_rel[:, :], float(P), None, ALU.subtract))
                chained(dve.tensor_scalar(dst_rel[:, :], dst_rel[:, :], span[:, :], None, ALU.add))
                first = dve.snap(seen, min_val=0, max_val=LAST)
                with dve.If(first < LAST):
                    with dve.Fori(first, LAST) as t:
                        step(as_tile(dve, t))
                dve.nop()
                t = LAST
                if layer == 0:
                    for k in range(t - 2, t + 1):
                        finish_first(k)
                else:
                    for k in range(t - 2, t + 1):
                        norm(k - 2)
                        take_stats(k)
                    norm(back(dve, t, 1))
                    norm(t)
                if layer < 2:
                    dve.wait_ge(own_made[layer], TILES + 2)
                    dve.sem_inc(layer_read, 1)

        @block.tensor
        def _(pe):
            pe.wait_ge(consts_made, 7)
            wide_zeros = zeros[:, :].rearrange("p (o n) -> p o n", o=1).to_broadcast([P, KD, P])

            pe.sem_inc(hots_counted, 2)
            pe.sem_inc(lo_made, SLOTS)
            pe.sem_inc(split_free, SPLIT)
            pe.sem_inc(pair_free, 2)
            for layer in range(3):
                pe.sem_inc(turned[layer], 1)
                pe.sem_inc(prod_free[layer], 2)
                pe.sem_inc(own_made[layer], 2)
            pe.matmul(count_ps[:, :], zeros[:, :], zeros[:, 0:TILES], start=True, stop=False)
            with pe.Fori(0, BODIES // 2) as i:
                for s in range(2):
                    pe.wait_ge(node_hot_made, i * 2 + (s + 1))
                    pe.wait_ge(tile_hot_made, i * 2 + (s + 1))
                    for c in range(BODY):
                        last = pe.matmul(count_ps[:, :], node_hot[s][:, c, :], tile_hot[s][:, c, :], start=False, stop=False)
                    last.then_inc(hots_counted, 1)
            pe.matmul(count_ps[:, :], zeros[:, :], zeros[:, 0:TILES], start=False, stop=True).then_inc(counted, 1)

            pe.wait_ge(ranges_loaded, 16)
            passes = passes_of(pe)
            cur = pe.alloc_register("pe_cur")
            for layer in range(3):
                weight = [weight_a, weight_b, weight_a][layer]

                def multiply(k):
                    pe.wait_ge(aggT_made[layer], k + 1)
                    pe.wait_ge(prod_free[layer], k + 1)
                    to = prod_ps[:, bass.ds(k % 2, 1), :]
                    for j in range(KD):
                        last = pe.matmul(to, aggT[:, j * P:(j + 1) * P], weight[:, j, :], start=(j == 0),
                                         stop=(j == KD - 1 and layer < 2))
                    if layer == 2:
                        for j in range(KD):
                            last = pe.matmul(to, pair[:, 1, j * P:(j + 1) * P], weight_b[:, j, :], start=False,
                                             stop=(j == KD - 1))
                    last.then_inc(prod_done[layer], 1)

                def turn(k):
                    pe.wait_ge(agg_taken[layer], k + 1)
                    if layer == 2:
                        pe.wait_ge(own_taken, k + 1)
                        for j in range(KD):
                            pe.transpose(turn2_ps[:, j * P:(j + 1) * P], pair[:, 0, j * P:(j + 1) * P], ident[:, :])
                    for j in range(KD):
                        last = pe.transpose(turn_ps[:, j * P:(j + 1) * P], agg_sb[:, j * P:(j + 1) * P], ident[:, :])
                    last.then_inc(turned[layer], 1)

                def close(t):
                    to = agg_ps[:, bass.ds(t % 2, 1), :]
                    if layer < 2:
                        last = pe.matmul(to, twice[:, :], own[:, bass.ds(t, 1), :], start=False, stop=True)
                    else:
                        last = pe.matmul(to, zeros[:, :], wide_zeros, start=False, stop=True)
                    last.then_inc(agg_done[layer], 1)

                def open_next(t):
                    pe.matmul(agg_ps[:, bass.ds((t + 1) % 2, 1), :], zeros[:, :], wide_zeros, start=True, stop=False)

                def finish(t):
                    with pe.If(t > 1):
                        multiply(back(pe, t, 2))
                    pe.nop()
                    with pe.If(t > 0):
                        turn(back(pe, t, 1))
                    pe.nop()
                    close(t)
                    open_next(t)

                def add_chunks(t, q, half, chunks):
                    to = agg_ps[:, bass.ds(t % 2, 1), :]
                    for c in chunks:
                        hot = onehot[:, q, c, half * P:(half + 1) * P]
                        pe.matmul(to, hot, part_hi[:, q, c * D:(c + 1) * D], start=False, stop=False)
                        last = pe.matmul(to, hot, part_lo[:, q, c * D:(c + 1) * D], start=False, stop=False)
                    return last

                pe.wait_ge(weights_loaded[layer], 32 if layer == 2 else 16)
                open_next(-1)
                pe.reg_mov(cur, 0)
                base = pe.snap(passes * (layer * BODIES * SLOTS))
                with pe.Fori(0, passes) as r:
                    with pe.Fori(0, BODIES) as i:
                        n = pe.snap(base + (r * BODIES + i) * SLOTS)
                        for s in range(SLOTS):
                            q = s % SPLIT
                            lo = lo_of(pe, i * SLOTS + s, r)
                            hi = hi_of(pe, i * SLOTS + s, r)
                            first = pe.snap(cur, min_val=0, max_val=LAST)
                            with pe.If(lo > first):
                                with pe.Fori(first, lo) as t:
                                    finish(as_tile(pe, t))
                            pe.nop()
                            pe.wait_ge(onehot_made, n + (s + 1))
                            pe.wait_ge(hi_made, n + (s + 1))
                            pe.wait_ge(lo_made, n + (s + 1 + SLOTS))
                            add_chunks(lo, q, 0, range(CHUNKS - 1))
                            with pe.If(hi > lo):
                                add_chunks(lo, q, 0, range(CHUNKS - 1, CHUNKS))
                                finish(lo)
                                add_chunks(hi, q, 1, range(CHUNKS)).then_inc(split_free, 1)
                            with pe.Else():
                                add_chunks(lo, q, 0, range(CHUNKS - 1, CHUNKS)).then_inc(split_free, 1)
                            pe.reg_mov(cur, hi)
                first = pe.snap(cur, min_val=0, max_val=LAST)
                with pe.If(first < LAST):
                    with pe.Fori(first, LAST) as t:
                        finish(as_tile(pe, t))
                pe.nop()
                multiply(LAST - 2)
                turn(LAST - 1)
                close(LAST)
                multiply(LAST - 1)
                turn(LAST)
                multiply(LAST)


def kernel(x, src, dst, L0_gnn_W1, L0_gnn_b1, L0_gnn_W2, L0_gnn_b2, L1_gnn_W_l, L1_gnn_b_l, L1_gnn_W_r):
    import numpy as np
    import concourse.bacc as bacc
    from concourse.bass_utils import run_bass_kernel_spmd

    x, src, dst = np.asarray(x), np.asarray(src), np.asarray(dst)
    n_nodes, n_edges = x.shape[0], src.shape[0]
    tiles = -(-n_nodes // P)
    bodies = 2 * -(-n_edges // (2 * BODY * P))
    edges = bodies * BODY * P
    x_rows = np.zeros((tiles * P, D), x.dtype)
    x_rows[:n_nodes] = x
    src_all = np.zeros(edges, src.dtype)
    src_all[:n_edges] = src
    dst_all = np.full(edges, n_nodes, dst.dtype)
    dst_all[:n_edges] = dst
    src_cols = src_all.reshape(-1, P).T
    arrays = {
        "x_rows": x_rows,
        "src_cols": np.concatenate([src_cols, src_cols[:, :BODY]], axis=1),
        "dst_cols": dst_all.reshape(-1, P).T,
        "dst_groups": dst_all.reshape(-1, GROUP),
        "w1": np.asarray(L0_gnn_W1), "b1": np.asarray(L0_gnn_b1).reshape(1, D),
        "w2": np.asarray(L0_gnn_W2), "b2": np.asarray(L0_gnn_b2).reshape(1, D),
        "wl": np.asarray(L1_gnn_W_l).T, "bl": np.asarray(L1_gnn_b_l).reshape(1, D),
        "wr": np.asarray(L1_gnn_W_r).T,
    }
    arrays = {k: np.ascontiguousarray(v) for k, v in arrays.items()}
    nc = bacc.Bacc("TRN2", target_bir_lowering=False, num_devices=1)
    args = [nc.dram_tensor(k, v.shape, mybir.dt.from_np(v.dtype), kind="ExternalInput").ap() for k, v in arrays.items()]
    out = nc.dram_tensor("y_rows", (tiles * P, D), mybir.dt.float32, kind="ExternalOutput").ap()
    gnn_program(nc, n_nodes, *args, out)
    result = run_bass_kernel_spmd(nc, [arrays], core_ids=[0])
    return result.results[0]["y_rows"][:n_nodes]
```

```python
from contextlib import ExitStack

import concourse.bass as bass
from concourse import mybir

P = 128
D = 512
KD = D // P
CHUNKS = 4
GROUP = CHUNKS * P
SLOTS = 4
BODY = SLOTS * CHUNKS
SPLIT = SLOTS
SUMS = 4
MINE = 8
RES = 4
STAGE = 21
EPS = 1e-5
SELF_LOOP_W = 2.0


def gnn_program(nc, n_nodes, x, src, dst, dst_groups, w1, b1, w2, b2, wl, bl, wr, out):
    fp32 = mybir.dt.float32
    fp32r = mybir.dt.float32r
    bf16 = mybir.dt.bfloat16
    i32 = mybir.dt.int32
    ALU = mybir.AluOpType
    ACT = mybir.ActivationFunctionType
    AX = mybir.AxisListType

    TILES = -(-n_nodes // P)
    ROWS = TILES * P
    GROUPS = dst_groups.shape[0]
    BODIES = GROUPS // SLOTS
    COLS = GROUPS * CHUNKS
    HALVES = -(-GROUPS // P)
    GROWS = GROUPS // HALVES
    LAST = TILES - 1
    assert n_nodes % P and GROUPS > 2 * SLOTS
    assert GROWS * HALVES == GROUPS and BODIES * SLOTS == GROUPS and TILES >= 6

    table = [nc.dram_tensor(f"table{n}", (ROWS, D), fp32, kind="Internal").ap() for n in range(3)]
    raw_dram = nc.dram_tensor("raw_ranges", (2, GROUPS), i32, kind="Internal").ap()
    range_dram = nc.dram_tensor("ranges_dram", (1, 2 * GROUPS + 1), i32, kind="Internal").ap()

    ctx = ExitStack()
    with ctx:
        def sb(name, shape, dt):
            return ctx.enter_context(nc.sbuf_tensor(name, shape, dt))

        def pb(name, shape, dt=fp32):
            return ctx.enter_context(nc.psum_tensor(name, shape, dt))

        def sem(name):
            return ctx.enter_context(nc.semaphore(name))

        mine = sb("mine", [P, MINE, D], fp32)
        stage = sb("stage", [P, STAGE, D], fp32)
        rows = sb("rows", [P, SLOTS, CHUNKS * D], fp32)
        part_hi = sb("part_hi", [P, SPLIT, CHUNKS * D], fp32r)
        part_lo = sb("part_lo", [P, SPLIT, CHUNKS * D], fp32r)
        onehot = sb("onehot", [P, SPLIT, CHUNKS, P], fp32r)
        onehot_next = sb("onehot_next", [P, CHUNKS, P], fp32r)
        weight_a = sb("weight_a", [P, KD, D], fp32)
        weight_b = sb("weight_b", [P, KD, D], fp32)
        bias = sb("bias", [P, D], fp32)
        agg_sb = sb("agg_sb", [P, D], fp32)
        aggT = sb("aggT", [P, D], fp32)
        pair = sb("pair", [P, 2, D], fp32)
        z = sb("z", [P, RES, D], fp32)
        dst_rel = sb("dst_rel", [P, COLS], fp32)
        src_slot = sb("src_slot", [P, SLOTS, CHUNKS], i32)
        window = sb("window", [P, 2 * P], bf16)
        ident = sb("ident", [P, P], fp32)
        twice = sb("twice", [P, P], fp32)
        zeros = sb("zeros", [P, P], bf16)
        span = sb("span", [P, 1], fp32)
        degree = sb("degree", [P, TILES], fp32)
        dinv = sb("dinv", [P, TILES], fp32)
        rmean = sb("rmean", [P, TILES], fp32)
        share = sb("share", [P, TILES], fp32)
        stats = sb("stats", [P, 6], fp32)
        moment = sb("moment", [P, 2], fp32)
        moments = sb("moments", [P, 2, 2], fp32)
        std = sb("std", [P, 2], fp32)
        rstd = sb("rstd", [P, 2], fp32)
        eps = sb("eps", [P, 1], fp32)
        ranges = sb("ranges", [1, 2 * GROUPS + 2], i32)

        rows_flat = rows[:, :, :].rearrange("p s f -> p (s f)")
        at = [0]

        def early(width, dt, size=4):
            a = at[0]
            at[0] = a + -(-width * size // 4)
            v = rows_flat[:, a:at[0]]
            return v if dt == fp32 else v.bitcast(dt)

        dst_g = early(HALVES * GROUP, i32).rearrange("p (a e) -> p a e", a=HALVES)
        dst_c = early(COLS, i32)
        dst_bits = early(COLS, i32)
        node_in_tile = early(COLS, fp32)
        tile_of = early(COLS, fp32)
        node_hot = [early(BODY * P, bf16, 2).rearrange("p (c n) -> p c n", c=BODY) for _ in range(2)]
        tile_hot = [early(BODY * TILES, bf16, 2).rearrange("p (c n) -> p c n", c=BODY) for _ in range(2)]
        assert at[0] <= SLOTS * CHUNKS * D
        z_flat = z[:, :, :].rearrange("p a f -> p (a f)")
        raw_i = z_flat[0:1, 0:2 * GROUPS].bitcast(i32)
        raw_f = z_flat[0:1, 2 * GROUPS:4 * GROUPS]
        assert 4 * GROUPS <= RES * D
        group_range = pair[:, 0, 0:2 * HALVES].bitcast(i32).rearrange("p (m a) -> p m a", m=2)
        range_i = pair[:, 1, 0:2 * HALVES].bitcast(i32).rearrange("p (m a) -> p m a", m=2)
        masked_f = agg_sb[0:1, 0:2 * GROUPS + 1] if 2 * GROUPS + 1 <= D else None
        masked_i = aggT[0:1, 0:2 * GROUPS + 1].bitcast(i32)
        steps_f = bias[0:1, 0:GROUPS]
        steps_g = bias[0:1, GROUPS:2 * GROUPS]
        worst = std[0:1, 0:1]
        worst2 = std[0:1, 1:2]
        keep = rstd[0:1, 0:1]
        lo_all = agg_sb[:, 0:GROUPS + 1]
        lo_raw = aggT[:, 0:GROUPS + 1].bitcast(i32)

        agg_ps = pb("agg_ps", [P, SUMS, D])
        turn_ps = pb("turn_ps", [P, D])
        turn2_ps = pb("turn2_ps", [P, D])
        prod_ps = pb("prod_ps", [P, 2, D])
        count_ps = turn2_ps[:, 0:TILES]

        consts_made = sem("consts_made")
        edges_loaded = sem("edges_loaded")
        group_rows_loaded = sem("group_rows_loaded")
        raw_stored = sem("raw_stored")
        raw_loaded = sem("raw_loaded")
        raw_made = sem("raw_made")
        masked_made = sem("masked_made")
        masked_stored = sem("masked_stored")
        ranges_loaded = sem("ranges_loaded")
        lo_loaded = sem("lo_loaded")
        dve_chain = sem("dve_chain")
        passed = sem("passed")
        digits_made = sem("digits_made")
        node_hot_made = sem("node_hot_made")
        tile_hot_made = sem("tile_hot_made")
        hots_counted = sem("hots_counted")
        counted = sem("counted")
        degree_made = sem("degree_made")
        root_made = sem("root_made")
        x_loaded = [sem(f"x_loaded{n}") for n in range(9)]
        x_stored = sem("x_stored")
        scaled = sem("scaled")
        rel_made = sem("rel_made")
        weights_loaded = [sem(f"weights_loaded{n}") for n in range(3)]
        bias_loaded = [sem(f"bias_loaded{n}") for n in range(3)]
        table_stored = [sem(f"table_stored{n}") for n in range(4)]
        layer_read = sem("layer_read")
        src_loaded = [sem(f"src_loaded{s}") for s in range(SLOTS)]
        gathered = [sem(f"gathered{s}") for s in range(SLOTS)]
        hi_made = sem("hi_made")
        lo_made = sem("lo_made")
        onehot_made = sem("onehot_made")
        split_free = sem("split_free")
        agg_done = [sem(f"agg_done{n}") for n in range(3)]
        agg_taken = [sem(f"agg_taken{n}") for n in range(3)]
        own_taken = sem("own_taken")
        mine_loaded = [sem(f"mine_loaded{n}") for n in range(3)]
        mine_free = sem("mine_free")
        onehot_next_made = sem("onehot_next_made")
        turned = [sem(f"turned{n}") for n in range(3)]
        aggT_made = [sem(f"aggT_made{n}") for n in range(3)]
        prod_done = [sem(f"prod_done{n}") for n in range(3)]
        prod_free = [sem(f"prod_free{n}") for n in range(3)]
        pair_loaded = sem("pair_loaded")
        pair_free = sem("pair_free")
        stats_made = [sem(f"stats_made{n}") for n in range(3)]
        std_made = [sem(f"std_made{n}") for n in range(3)]
        own_made = [sem(f"own_made{n}") for n in range(3)]

        tiles = []
        scale_of = [dinv, dinv, rmean]
        stored_to = [table[1], table[2], out]

        def passes_of(eng):
            return eng.value_load(ranges[0:1, 2 * GROUPS:2 * GROUPS + 1], min_val=1, max_val=TILES)

        def stand_alone(eng):
            eng.sem_inc(passed, 1)

        def as_tile(eng, value):
            tile = eng.alloc_register(f"tile{len(tiles)}")
            tiles.append(tile)
            eng.reg_mov(tile, value)
            return eng.snap(tile, min_val=0, max_val=LAST)

        def lo_of(eng, g, r):
            return as_tile(eng, eng.value_load(ranges[0:1, bass.ds(g, 1)], min_val=0, max_val=LAST) + r)

        def hi_of(eng, g, r):
            return as_tile(eng, eng.value_load(ranges[0:1, bass.ds(GROUPS + g, 1)], min_val=0, max_val=LAST) + r)

        def ahead(eng, t, k):
            return as_tile(eng, t + k)

        def back(eng, t, k):
            if isinstance(t, int):
                return t - k
            tile = eng.alloc_register(f"tile{len(tiles)}")
            tiles.append(tile)
            eng.reg_alu(tile, eng.snap(t - k), 0, ALU.max)
            return eng.snap(tile, min_val=0, max_val=LAST)

        in_rows = rows_flat.rearrange("p (t f) -> p t f", f=D)
        pieces = []
        for a0, a1, place, shift in ((0, STAGE, stage, 0), (STAGE, STAGE + 16, in_rows, STAGE),
                                     (STAGE + 16, TILES, stage, STAGE + 16)):
            a1 = min(a1, TILES)
            for a in range(a0, a1, 7):
                b = min(a + 7, a1)
                pieces.append((a, b, place[:, a - shift:b - shift, :], place is in_rows, a0 > STAGE))
        FIRST = min(2, len(pieces))
        assert len(pieces) <= 9 and TILES <= STAGE + 16 + 14 <= 2 * STAGE + 16

        def load_piece(eng, n):
            a, b, place, _, _ = pieces[n]
            eng.dma_start(place, x[a * P:b * P, :].rearrange("(t p) f -> p t f", p=P)).then_inc(x_loaded[n], 16)

        block = ctx.enter_context(nc.Block())

        @block.sync
        def _(sp):
            sp.dma_start(dst_g[0:GROWS], dst_groups.rearrange("(a p) e -> p a e", p=GROWS)).then_inc(group_rows_loaded, 16)
            sp.dma_start(dst_c, dst).then_inc(edges_loaded, 16)
            for s in range(SLOTS):
                sp.dma_start(src_slot[:, s, :], src[:, s * CHUNKS:(s + 1) * CHUNKS]).then_inc(src_loaded[s], 16)
            sp.wait_ge(raw_made, 1)
            sp.dma_start(raw_dram.rearrange("m (a p) -> p m a", p=GROWS), range_i[0:GROWS],
                         allow_slow_non_contiguous=True).then_inc(raw_stored, 16)
            sp.wait_ge(raw_stored, 16)
            sp.dma_start(raw_i, raw_dram.rearrange("m (o g) -> o (m g)", o=1)).then_inc(raw_loaded, 16)
            sp.wait_ge(masked_made, 1)
            sp.dma_start(range_dram, masked_i).then_inc(masked_stored, 16)
            sp.wait_ge(masked_stored, 16)
            sp.dma_start(ranges[0:1, 0:2 * GROUPS + 1], range_dram).then_inc(ranges_loaded, 16)
            sp.dma_start(lo_raw[:, 0:GROUPS], range_dram[0:1, 0:GROUPS].to_broadcast([P, GROUPS]))\
              .then_inc(lo_loaded, 16)
            sp.dma_start(lo_raw[:, GROUPS:GROUPS + 1], range_dram[0:1, 2 * GROUPS:2 * GROUPS + 1].to_broadcast([P, 1]))\
              .then_inc(lo_loaded, 16)
            for n, (_, _, _, late, again) in enumerate(pieces):
                if not late and not again:
                    load_piece(sp, n)
            sp.dma_start(weight_a[:, :, :], w1.rearrange("(k p) n -> p k n", p=P)).then_inc(weights_loaded[0], 16)
            sp.dma_start(weight_b[:, :, :], w2.rearrange("(k p) n -> p k n", p=P)).then_inc(weights_loaded[1], 16)
            sp.wait_ge(counted, 1)
            sp.wait_ge(rel_made, 1)
            for n, (_, _, _, late, _) in enumerate(pieces):
                if late:
                    load_piece(sp, n)
            for n, (_, _, _, _, again) in enumerate(pieces):
                if again:
                    sp.wait_ge(x_stored, 32)
                    load_piece(sp, n)
            sp.wait_ge(ranges_loaded, 16)
            passes = passes_of(sp)
            for layer, b in enumerate((b1, b2, bl)):
                sp.wait_ge(layer_read, layer + 1)
                sp.dma_start(bias[:, :], b.to_broadcast([P, D])).then_inc(bias_loaded[layer], 16)
                if layer == 1:
                    sp.dma_start(weight_a[:, :, :], wl.rearrange("(k p) n -> p k n", p=P))\
                      .then_inc(weights_loaded[2], 16)
                if layer == 2:
                    sp.dma_start(weight_b[:, :, :], wr.rearrange("(k p) n -> p k n", p=P))\
                      .then_inc(weights_loaded[2], 16)
                base = sp.snap(passes * (layer * BODIES))
                with sp.Fori(0, passes) as r:
                    with sp.Fori(0, BODIES) as i:
                        n = sp.snap(base + r * BODIES + i + 1)
                        for s in range(SLOTS):
                            sp.wait_ge(gathered[s], n * (16 * CHUNKS))
                            sp.dma_start(src_slot[:, s, :], src[:, bass.ds(i * BODY + BODY + s * CHUNKS, CHUNKS)])\
                              .then_inc(src_loaded[s], 16)
            for s in range(SLOTS):
                sp.wait_ge(src_loaded[s], sp.snap(passes * (3 * BODIES * 16) + 16))
            stand_alone(sp)

        @block.gpsimd
        def _(pool):
            pool.iota(window[:, :], pattern=[[1, 2 * P]], base=0, channel_multiplier=0,
                      allow_small_or_imprecise_dtypes=True).then_inc(consts_made, 1)
            pool.memset(zeros[:, :], 0.0).then_inc(consts_made, 1)
            pool.memset(eps[:, :], EPS).then_inc(consts_made, 1)
            pool.memset(ident[:, :], 0.0).then_inc(consts_made, 1)
            pool.memset(twice[:, :], 0.0).then_inc(consts_made, 1)
            pool.wait_ge(consts_made, 5)
            for m, v in ((ident, 1.0), (twice, SELF_LOOP_W)):
                pool.affine_select(out=m[:, :], in_=m[:, :], compare_op=ALU.not_equal, fill=v, base=0,
                                   pattern=[[-1, P]], channel_multiplier=1).then_inc(consts_made, 1)
            pool.wait_ge(ranges_loaded, 16)
            passes = passes_of(pool)
            for layer in range(3):
                if layer == 0:
                    pool.wait_ge(x_stored, 16 * FIRST)
                pool.wait_ge(table_stored[layer], 16 * (len(pieces) - FIRST if layer == 0 else TILES + RES))
                base = pool.snap(passes * (layer * BODIES))
                with pool.Fori(0, passes) as r:
                    with pool.Fori(0, BODIES) as i:
                        n = pool.snap(base + r * BODIES + i)
                        for s in range(SLOTS):
                            pool.wait_ge(src_loaded[s], n * 16 + 16)
                            pool.wait_ge(lo_made, n * SLOTS + (s + 1))
                            stand_alone(pool)
                            for c in range(CHUNKS):
                                pool.indirect_dma_start(
                                    rows[:, s, c * D:(c + 1) * D], None, table[layer],
                                    bass.IndirectOffsetOnAxis(ap=src_slot[:, s, c:c + 1], axis=0))\
                                    .then_inc(gathered[s], 16)

        @block.scalar
        def _(act):
            act.wait_ge(consts_made, 7)
            act.wait_ge(degree_made, 1)
            act.activation(degree[:, :], degree[:, :], ACT.Sqrt).then_inc(root_made, 1)
            for n, (a, b, place, _, _) in enumerate(pieces):
                act.wait_ge(scaled, n + 1)
                act.dma_start(table[0][a * P:b * P, :].rearrange("(t p) f -> p t f", p=P), place)\
                   .then_inc(x_stored if n < FIRST else table_stored[0], 16)
            act.wait_ge(ranges_loaded, 16)
            passes = passes_of(act)
            seen = act.alloc_register("act_seen")
            for layer in range(3):
                normed = layer > 0

                def take_sums(t):
                    act.wait_ge(turned[layer], t + 1)
                    if layer == 2:
                        act.wait_ge(mine_loaded[layer], t * 16 + 16)
                        act.activation(pair[:, 0, :], mine[:, bass.ds(t % MINE, 1), :], ACT.Copy).then_inc(own_taken, 1)
                    act.wait_ge(agg_done[layer], t + 1)
                    act.activation(agg_sb[:, :], agg_ps[:, bass.ds(t % SUMS, 1), :], ACT.Identity,
                                   scale=scale_of[layer][:, bass.ds(t, 1)]).then_inc(agg_taken[layer], 1)

                def take_turned(k):
                    act.wait_ge(turned[layer], k + 2)
                    if layer == 2:
                        act.activation(pair[:, 1, :], turn2_ps[:, :], ACT.Copy)
                    act.activation(aggT[:, :], turn_ps[:, :], ACT.Copy).then_inc(aggT_made[layer], 1)

                def take_root(k):
                    act.wait_ge(stats_made[layer], k + 1)
                    act.activation(std[:, bass.ds(k % 2, 1)], moments[:, bass.ds(k % 2, 1), 1:2], ACT.Sqrt,
                                   bias=eps[:, 0:1]).then_inc(std_made[layer], 1)

                def load_x(k):
                    act.wait_ge(pair_free, k + 1)
                    act.dma_start(pair[:, bass.ds(k % 2, 1), :], x[bass.ds(k * P, P), :]).then_inc(pair_loaded, 16)

                def load_mine(k):
                    act.wait_ge(mine_loaded[layer], k * 16)
                    if layer == 2:
                        act.wait_ge(mine_free, k + 1)
                    act.dma_start(mine[:, bass.ds(k % MINE, 1), :], table[layer][bass.ds(k * P, P), :])\
                       .then_inc(mine_loaded[layer], 16)

                def store(k):
                    act.wait_ge(own_made[layer], k + 1)
                    act.wait_ge(table_stored[layer + 1], k * 16 + 16 * RES)
                    act.dma_start(stored_to[layer][bass.ds(k * P, P), :], z[:, bass.ds(k % RES, 1), :])\
                       .then_inc(table_stored[layer + 1], 16)

                def step(t):
                    with act.If(t > 0):
                        take_turned(back(act, t, 1))
                    act.nop()
                    take_sums(t)
                    with act.If(t < LAST - 1):
                        load_mine(ahead(act, t, 2))
                    act.nop()
                    if layer == 1:
                        with act.If(t > 1):
                            k = back(act, t, 1)
                            act.wait_ge(pair_loaded, k * 16)
                            load_x(k)
                        act.nop()
                    if normed:
                        with act.If(t > 2):
                            take_root(back(act, t, 3))
                        act.nop()
                        with act.If(t > 4):
                            store(back(act, t, 5))
                        act.nop()
                    else:
                        with act.If(t > 2):
                            store(back(act, t, 3))
                        act.nop()

                if layer == 1:
                    act.dma_start(pair[:, 0, :], x[0:P, :]).then_inc(pair_loaded, 16)
                if layer == 0:
                    act.wait_ge(x_stored, 16 * FIRST)
                act.wait_ge(table_stored[layer], 16 * (len(pieces) - FIRST if layer == 0 else TILES + RES))
                act.dma_start(mine[:, 0, :], table[layer][0:P, :]).then_inc(mine_loaded[layer], 16)
                act.wait_ge(mine_loaded[layer], 16)
                act.dma_start(mine[:, 1, :], table[layer][P:2 * P, :]).then_inc(mine_loaded[layer], 16)
                act.reg_mov(seen, 0)
                base = act.snap(passes * (layer * BODIES * SLOTS))
                before = [act.alloc_register(f"act_before{layer}_{s}") for s in range(SLOTS)]
                for s in range(SLOTS):
                    act.reg_mov(before[s], 0)
                with act.Fori(0, passes) as r:
                    with act.Fori(0, BODIES) as i:
                        n = act.snap(base + (r * BODIES + i) * SLOTS)
                        m = act.snap((passes * (layer * BODIES) + r * BODIES + i + 1) * (16 * CHUNKS))
                        for s in range(SLOTS):
                            act.wait_ge(split_free, n + (s + 1))
                            act.wait_ge(gathered[s], m)
                            act.activation(part_hi[:, s % SPLIT, :], rows[:, s, :], ACT.Copy).then_inc(hi_made, 1)
                            done = act.snap(before[s], min_val=0, max_val=LAST)
                            first = act.snap(seen, min_val=0, max_val=LAST)
                            with act.If(done > first):
                                with act.Fori(first, done) as t:
                                    step(as_tile(act, t))
                                act.reg_mov(seen, done)
                            act.reg_mov(before[s], hi_of(act, i * SLOTS + s, r))
                first = act.snap(seen, min_val=0, max_val=LAST)
                with act.If(first < LAST):
                    with act.Fori(first, LAST) as t:
                        step(as_tile(act, t))
                act.nop()
                t = LAST
                take_turned(t - 1)
                take_sums(t)
                if layer == 1:
                    act.wait_ge(pair_loaded, 16 * (t - 1))
                    load_x(back(act, t, 1))
                    act.wait_ge(pair_loaded, 16 * t)
                    load_x(t)
                if normed:
                    take_root(back(act, t, 3))
                    store(back(act, t, 5))
                take_turned(t)
                if normed:
                    for k in range(t - 2, t + 1):
                        take_root(k)
                        store(k - 2)
                    store(back(act, t, 1))
                    store(t)
                else:
                    for k in range(t - 3, t + 1):
                        store(k)
            act.wait_ge(table_stored[3], 16 * (TILES + RES))

        @block.vector
        def _(dve):
            chain = [0]

            def link(ins):
                chain[0] += 1
                ins.then_inc(dve_chain, 1)
                dve.wait_ge(dve_chain, chain[0])

            dve.wait_ge(group_rows_loaded, 16)
            link(dve.tensor_reduce(group_range[0:GROWS, 0, :], dst_g[0:GROWS], AX.X, ALU.min))
            link(dve.tensor_reduce(group_range[0:GROWS, 1, :], dst_g[0:GROWS], AX.X, ALU.max))
            dve.tensor_scalar(range_i[0:GROWS], group_range[0:GROWS], 7, None, ALU.arith_shift_right)\
               .then_inc(raw_made, 1)
            dve.wait_ge(edges_loaded, 16)
            link(dve.tensor_scalar(dst_bits, dst_c, P - 1, None, ALU.bitwise_and))
            link(dve.tensor_copy(node_in_tile, dst_bits))
            link(dve.tensor_scalar(dst_bits, dst_c, 7, None, ALU.arith_shift_right))
            dve.tensor_copy(tile_of, dst_bits).then_inc(digits_made, 1)
            dve.tensor_copy(dst_rel[:, :], dst_c).then_inc(digits_made, 1)
            dve.wait_ge(consts_made, 7)
            dve.wait_ge(digits_made, 2)
            with dve.Fori(0, BODIES // 2) as i:
                for s in range(2):
                    dve.wait_ge(hots_counted, i * 2 + (s + 1))
                    for c in range(BODY):
                        made = dve.tensor_scalar(node_hot[s][:, c, :], window[:, 0:P],
                                                 node_in_tile[:, bass.ds((i * 2 + s) * BODY + c, 1)], None, ALU.is_equal)
                    made.then_inc(node_hot_made, 1)
                    dve.tensor_tensor(
                        tile_hot[s][:, :, :],
                        window[:, 0:TILES].rearrange("p (o n) -> p o n", o=1).to_broadcast([P, BODY, TILES]),
                        tile_of[:, bass.ds((i * 2 + s) * BODY, BODY)].rearrange("p (c o) -> p c o", o=1)
                        .to_broadcast([P, BODY, TILES]),
                        ALU.is_equal).then_inc(tile_hot_made, 1)
            dve.wait_ge(raw_loaded, 16)
            link(dve.tensor_copy(raw_f, raw_i))
            lo_f, hi_f = raw_f[:, 0:GROUPS], raw_f[:, GROUPS:2 * GROUPS]
            link(dve.tensor_tensor(steps_f, hi_f, lo_f, ALU.subtract))
            link(dve.tensor_reduce(worst, steps_f, AX.X, ALU.max))
            link(dve.tensor_tensor(steps_g[:, 0:GROUPS - 1], hi_f[:, 0:GROUPS - 1], lo_f[:, 1:GROUPS], ALU.subtract))
            link(dve.tensor_reduce(worst2, steps_g[:, 0:GROUPS - 1], AX.X, ALU.max))
            link(dve.tensor_scalar(worst, worst, 1.0, None, ALU.subtract))
            link(dve.tensor_tensor(worst, worst, worst2, ALU.max))
            link(dve.tensor_reduce(worst2, steps_g[:, 0:GROUPS - 1], AX.X, ALU.min))
            link(dve.tensor_scalar(worst2, worst2, -1.0, -1.0, ALU.mult, ALU.add))
            link(dve.tensor_tensor(worst, worst, worst2, ALU.max))
            reach = SLOTS + 1
            link(dve.tensor_tensor(steps_f[:, 0:GROUPS - reach], hi_f[:, reach:GROUPS], hi_f[:, 0:GROUPS - reach],
                                   ALU.subtract))
            link(dve.tensor_reduce(worst2, steps_f[:, 0:GROUPS - reach], AX.X, ALU.max))
            link(dve.tensor_tensor(worst2, worst2, hi_f[:, reach - 1:reach], ALU.max))
            link(dve.tensor_scalar(worst2, worst2, 3.0, None, ALU.subtract))
            link(dve.tensor_tensor(worst, worst, worst2, ALU.max))
            link(dve.tensor_tensor(worst, worst, lo_f[:, 0:1], ALU.max))
            link(dve.tensor_scalar(keep, worst, 1.0, None, ALU.is_lt))
            link(dve.tensor_scalar(masked_f[:, 0:2 * GROUPS], raw_f, keep, None, ALU.mult))
            link(dve.tensor_scalar(masked_f[:, 2 * GROUPS:2 * GROUPS + 1], keep, -float(TILES - 1), float(TILES),
                                   ALU.mult, ALU.add))
            dve.tensor_copy(masked_i, masked_f).then_inc(masked_made, 1)
            dve.wait_ge(counted, 1)
            link(dve.tensor_copy(rmean[:, :], count_ps))
            dve.tensor_scalar(degree[:, :], rmean[:, :], SELF_LOOP_W, None, ALU.add).then_inc(degree_made, 1)
            link(dve.tensor_scalar(dinv[:, :], rmean[:, :], 1.0, None, ALU.max))
            link(dve.tensor_copy(share[:, :], rmean[:, :]))
            link(dve.reciprocal(rmean[:, :], dinv[:, :]))
            link(dve.tensor_tensor(share[:, :], share[:, :], rmean[:, :], ALU.mult))
            dve.wait_ge(root_made, 1)
            link(dve.reciprocal(dinv[:, :], degree[:, :]))
            dve.wait_ge(lo_loaded, 32)
            link(dve.tensor_copy(lo_all, lo_raw))
            link(dve.tensor_scalar(lo_all, lo_all, float(P), None, ALU.mult))
            rel = dst_rel[:, :].rearrange("p (g c) -> p g c", c=CHUNKS)
            link(dve.tensor_tensor(rel, rel, lo_all[:, 0:GROUPS].rearrange("p (g o) -> p g o", o=1)
                                   .to_broadcast([P, GROUPS, CHUNKS]), ALU.subtract))
            dve.sem_inc(rel_made, 1)
            dve.tensor_copy(span[:, :], lo_all[:, GROUPS:GROUPS + 1])
            for n, (a, b, place, _, _) in enumerate(pieces):
                dve.wait_ge(x_loaded[n], 16)
                for t in range(a, b):
                    last = dve.tensor_scalar(place[:, t - a, :], place[:, t - a, :], dinv[:, t:t + 1], None, ALU.mult)
                last.then_inc(scaled, 1)
            dve.sem_inc(layer_read, 1)
            dve.wait_ge(ranges_loaded, 16)
            passes = passes_of(dve)
            seen = dve.alloc_register("dve_seen")
            links = dve.alloc_register("dve_links")
            linked = sem("linked")
            dve.reg_mov(links, 0)
            next_used = dve.alloc_register("dve_next_used")
            dve.reg_mov(next_used, SPLIT)
            for layer in range(3):
                def chained(ins):
                    ins.then_inc(linked, 1)
                    v = dve.snap(dve.snap(links) + 1)
                    dve.reg_mov(links, v)
                    dve.wait_ge(linked, v)
                    stand_alone(dve)

                def take_product(k):
                    dve.wait_ge(prod_done[layer], k + 1)
                    dve.wait_ge(table_stored[layer + 1], k * 16 + 16)
                    zk = z[:, bass.ds(k % RES, 1), :]
                    pk = prod_ps[:, bass.ds(k % 2, 1), :]
                    bk = bias[:, :].rearrange("p (o f) -> p o f", o=1)
                    if layer < 2:
                        ins = dve.tensor_tensor(zk, pk, bk, ALU.add)
                    else:
                        ins = dve.scalar_tensor_tensor(out=zk, in0=bk, scalar=share[:, bass.ds(k, 1)], in1=pk,
                                                       op0=ALU.mult, op1=ALU.add)
                    ins.then_inc(prod_free[layer], 1)
                    dve.wait_ge(prod_free[layer], k + 3)

                def finish_first(k):
                    take_product(k)
                    zk = z[:, bass.ds(k % RES, 1), :]
                    dve.tensor_scalar(zk, zk, 0.0,
                                      dinv[:, bass.ds(k, 1)], ALU.max, ALU.mult).then_inc(own_made[layer], 1)

                def take_stats(k):
                    take_product(k)
                    zk = z[:, bass.ds(k % RES, 1), :]
                    if layer == 1:
                        dve.wait_ge(pair_loaded, k * 16 + 16)
                        ins = dve.scalar_tensor_tensor(out=zk, in0=zk, scalar=0.0, in1=pair[:, bass.ds(k % 2, 1), :],
                                                       op0=ALU.max, op1=ALU.add)
                        ins.then_inc(pair_free, 1)
                        dve.wait_ge(pair_free, k + 3)
                        stand_alone(dve)
                    else:
                        dve.tensor_tensor(zk, zk, mine[:, bass.ds(k % MINE, 1), :], ALU.add).then_inc(mine_free, 1)
                        dve.wait_ge(mine_free, k + (1 + MINE))
                        stand_alone(dve)
                    chained(dve.bn_stats(stats[:, :], z[:, bass.ds(k % RES, 1), :]))
                    chained(dve.bn_aggr(moment[:, :], stats[:, :]))
                    dve.tensor_copy(moments[:, bass.ds(k % 2, 1), :], moment[:, :]).then_inc(stats_made[layer], 1)

                def norm(k):
                    dve.wait_ge(std_made[layer], k + 1)
                    chained(dve.reciprocal(rstd[:, bass.ds(k % 2, 1)], std[:, bass.ds(k % 2, 1)]))
                    zk = z[:, bass.ds(k % RES, 1), :]
                    dve.tensor_scalar(zk, zk,
                                      moments[:, bass.ds(k % 2, 1), 0:1], rstd[:, bass.ds(k % 2, 1)],
                                      ALU.subtract, ALU.mult).then_inc(own_made[layer], 1)

                def step(t):
                    if layer == 0:
                        with dve.If(t > 1):
                            finish_first(back(dve, t, 2))
                        dve.nop()
                    else:
                        with dve.If(t > 3):
                            norm(back(dve, t, 4))
                        dve.nop()
                        with dve.If(t > 1):
                            take_stats(back(dve, t, 2))
                        dve.nop()

                dve.wait_ge(bias_loaded[layer], 16)
                dve.reg_mov(seen, 0)
                before = [dve.alloc_register(f"dve_before{layer}_{s}") for s in range(SLOTS)]
                for s in range(SLOTS):
                    dve.reg_mov(before[s], 0)
                base = dve.snap(passes * (layer * BODIES * SLOTS))
                with dve.Fori(0, passes) as r:
                    with dve.Fori(0, BODIES) as i:
                        n = dve.snap(base + (r * BODIES + i) * SLOTS)
                        for s in range(SLOTS):
                            dve.wait_ge(split_free, n + (s + 1))
                            for c in range(CHUNKS):
                                made = dve.tensor_scalar(onehot[:, s % SPLIT, c, :], window[:, 0:P],
                                                         dst_rel[:, bass.ds(i * BODY + (s * CHUNKS + c), 1)], None,
                                                         ALU.is_equal)
                            made.then_inc(onehot_made, 1)
                            lo = lo_of(dve, i * SLOTS + s, r)
                            hi = hi_of(dve, i * SLOTS + s, r)
                            with dve.If(hi > lo):
                                dve.wait_ge(split_free, dve.snap(next_used))
                                for c in range(CHUNKS):
                                    made = dve.tensor_scalar(onehot_next[:, c, :], window[:, P:2 * P],
                                                             dst_rel[:, bass.ds(i * BODY + (s * CHUNKS + c), 1)], None,
                                                             ALU.is_equal)
                                made.then_inc(onehot_next_made, 1)
                                dve.reg_mov(next_used, dve.snap(n + (s + 1 + SPLIT)))
                            dve.wait_ge(hi_made, n + (s + 1))
                            dve.tensor_tensor(part_lo[:, s % SPLIT, :], rows[:, s, :], part_hi[:, s % SPLIT, :],
                                              ALU.subtract).then_inc(lo_made, 1)
                            done = dve.snap(before[s], min_val=0, max_val=LAST)
                            first = dve.snap(seen, min_val=0, max_val=LAST)
                            with dve.If(done > first):
                                with dve.Fori(first, done) as t:
                                    step(as_tile(dve, t))
                                dve.reg_mov(seen, done)
                            dve.reg_mov(before[s], hi)
                    dve.wait_ge(onehot_made, dve.snap(base + r * GROUPS + GROUPS))
                    chained(dve.tensor_scalar(dst_rel[:, :], dst_rel[:, :], float(P), None, ALU.subtract))
                chained(dve.tensor_scalar(dst_rel[:, :], dst_rel[:, :], span[:, :], None, ALU.add))
                first = dve.snap(seen, min_val=0, max_val=LAST)
                with dve.If(first < LAST):
                    with dve.Fori(first, LAST) as t:
                        step(as_tile(dve, t))
                dve.nop()
                t = LAST
                if layer == 0:
                    for k in range(t - 2, t + 1):
                        finish_first(k)
                else:
                    for k in range(t - 2, t + 1):
                        norm(k - 2)
                        take_stats(k)
                    norm(back(dve, t, 1))
                    norm(t)
                if layer < 2:
                    dve.wait_ge(own_made[layer], TILES)
                    dve.sem_inc(layer_read, 1)

        @block.tensor
        def _(pe):
            pe.wait_ge(consts_made, 7)
            wide_zeros = zeros[:, :].rearrange("p (o n) -> p o n", o=1).to_broadcast([P, KD, P])

            pe.sem_inc(hots_counted, 2)
            pe.sem_inc(lo_made, SLOTS)
            pe.sem_inc(split_free, SPLIT)
            pe.sem_inc(pair_free, 2)
            pe.sem_inc(mine_free, MINE)
            for layer in range(3):
                pe.sem_inc(turned[layer], 1)
                pe.sem_inc(agg_taken[layer], SUMS - 1)
                pe.sem_inc(prod_free[layer], 2)
                pe.sem_inc(table_stored[layer + 1], 16 * RES)
            pe.matmul(count_ps, zeros[:, :], zeros[:, 0:TILES], start=True, stop=False)
            with pe.Fori(0, BODIES // 2) as i:
                for s in range(2):
                    pe.wait_ge(node_hot_made, i * 2 + (s + 1))
                    pe.wait_ge(tile_hot_made, i * 2 + (s + 1))
                    for c in range(BODY):
                        last = pe.matmul(count_ps, node_hot[s][:, c, :], tile_hot[s][:, c, :], start=False, stop=False)
                    last.then_inc(hots_counted, 1)
            pe.matmul(count_ps, zeros[:, :], zeros[:, 0:TILES], start=False, stop=True).then_inc(counted, 1)

            pe.wait_ge(ranges_loaded, 16)
            passes = passes_of(pe)
            cur = pe.alloc_register("pe_cur")
            seen = pe.alloc_register("pe_seen")
            met_two = pe.alloc_register("pe_met_two")
            pe.reg_mov(met_two, 0)
            for layer in range(3):
                weight = [weight_a, weight_b, weight_a][layer]

                def multiply(k):
                    pe.wait_ge(aggT_made[layer], k + 1)
                    pe.wait_ge(prod_free[layer], k + 1)
                    to = prod_ps[:, bass.ds(k % 2, 1), :]
                    for j in range(KD):
                        last = pe.matmul(to, aggT[:, j * P:(j + 1) * P], weight[:, j, :], start=(j == 0),
                                         stop=(j == KD - 1 and layer < 2))
                    if layer == 2:
                        for j in range(KD):
                            last = pe.matmul(to, pair[:, 1, j * P:(j + 1) * P], weight_b[:, j, :], start=False,
                                             stop=(j == KD - 1))
                    last.then_inc(prod_done[layer], 1)

                def turn(k):
                    pe.wait_ge(agg_taken[layer], k + SUMS)
                    if layer == 2:
                        pe.wait_ge(own_taken, k + 1)
                        for j in range(KD):
                            pe.transpose(turn2_ps[:, j * P:(j + 1) * P], pair[:, 0, j * P:(j + 1) * P], ident[:, :])
                    for j in range(KD):
                        last = pe.transpose(turn_ps[:, j * P:(j + 1) * P], agg_sb[:, j * P:(j + 1) * P], ident[:, :])
                    last.then_inc(turned[layer], 1)

                def close(t):
                    to = agg_ps[:, bass.ds(t % SUMS, 1), :]
                    if layer < 2:
                        pe.wait_ge(mine_loaded[layer], t * 16 + 16)
                        last = pe.matmul(to, twice[:, :], mine[:, bass.ds(t % MINE, 1), :], start=False, stop=True)
                    else:
                        last = pe.matmul(to, zeros[:, :], wide_zeros, start=False, stop=True)
                    last.then_inc(agg_done[layer], 1)

                def open_next(t):
                    if not isinstance(t, int):
                        pe.wait_ge(agg_taken[layer], t + 1)
                    bank = (t + 1) % SUMS
                    pe.matmul(agg_ps[:, bass.ds(bank, 1), :], zeros[:, :], wide_zeros, start=True, stop=False)

                def finish(t):
                    close(t)
                    open_next(t)

                def step(t):
                    with pe.If(t > 0):
                        multiply(back(pe, t, 1))
                    pe.nop()
                    turn(t)

                def add_chunks(t, q, hots, chunks):
                    to = agg_ps[:, bass.ds(t % SUMS, 1), :]
                    for c in chunks:
                        hot = hots[:, c, :]
                        pe.matmul(to, hot, part_hi[:, q, c * D:(c + 1) * D], start=False, stop=False)
                        last = pe.matmul(to, hot, part_lo[:, q, c * D:(c + 1) * D], start=False, stop=False)
                    return last

                pe.wait_ge(weights_loaded[layer], 32 if layer == 2 else 16)
                open_next(-1)
                pe.reg_mov(cur, 0)
                pe.reg_mov(seen, 0)
                before = [pe.alloc_register(f"pe_before{layer}_{s}") for s in range(SLOTS)]
                for s in range(SLOTS):
                    pe.reg_mov(before[s], 0)
                base = pe.snap(passes * (layer * BODIES * SLOTS))
                with pe.Fori(0, passes) as r:
                    with pe.Fori(0, BODIES) as i:
                        n = pe.snap(base + (r * BODIES + i) * SLOTS)
                        for s in range(SLOTS):
                            q = s % SPLIT
                            lo = lo_of(pe, i * SLOTS + s, r)
                            hi = hi_of(pe, i * SLOTS + s, r)
                            first = pe.snap(cur, min_val=0, max_val=LAST)
                            with pe.If(lo > first):
                                with pe.Fori(first, lo) as t:
                                    finish(as_tile(pe, t))
                            pe.nop()
                            pe.wait_ge(onehot_made, n + (s + 1))
                            pe.wait_ge(hi_made, n + (s + 1))
                            pe.wait_ge(lo_made, n + (s + 1 + SLOTS))
                            add_chunks(lo, q, onehot[:, q], range(CHUNKS - 1))
                            with pe.If(hi > lo):
                                add_chunks(lo, q, onehot[:, q], range(CHUNKS - 1, CHUNKS))
                                finish(lo)
                                v = pe.snap(pe.snap(met_two) + 1)
                                pe.reg_mov(met_two, v)
                                pe.wait_ge(onehot_next_made, v)
                                last = add_chunks(hi, q, onehot_next, range(CHUNKS))
                                last.then_inc(split_free, 1)
                            with pe.Else():
                                add_chunks(lo, q, onehot[:, q], range(CHUNKS - 1, CHUNKS)).then_inc(split_free, 1)
                            pe.reg_mov(cur, hi)
                            done = pe.snap(before[s], min_val=0, max_val=LAST)
                            first = pe.snap(seen, min_val=0, max_val=LAST)
                            with pe.If(done > first):
                                with pe.Fori(first, done) as t:
                                    step(as_tile(pe, t))
                                pe.reg_mov(seen, done)
                            pe.reg_mov(before[s], hi)
                close(LAST)
                first = pe.snap(seen, min_val=0, max_val=LAST)
                with pe.If(first < LAST):
                    with pe.Fori(first, LAST) as t:
                        step(as_tile(pe, t))
                pe.nop()
                multiply(LAST - 1)
                turn(LAST)
                multiply(LAST)


def kernel(x, src, dst, L0_gnn_W1, L0_gnn_b1, L0_gnn_W2, L0_gnn_b2, L1_gnn_W_l, L1_gnn_b_l, L1_gnn_W_r):
    import numpy as np
    import concourse.bacc as bacc
    from concourse.bass_utils import run_bass_kernel_spmd

    x, src, dst = np.asarray(x), np.asarray(src), np.asarray(dst)
    n_nodes, n_edges = x.shape[0], src.shape[0]
    tiles = -(-n_nodes // P)
    bodies = 2 * -(-n_edges // (2 * BODY * P))
    edges = bodies * BODY * P
    x_rows = np.zeros((tiles * P, D), x.dtype)
    x_rows[:n_nodes] = x
    src_all = np.zeros(edges, src.dtype)
    src_all[:n_edges] = src
    dst_all = np.full(edges, n_nodes, dst.dtype)
    dst_all[:n_edges] = dst
    src_cols = src_all.reshape(-1, P).T
    arrays = {
        "x_rows": x_rows,
        "src_cols": np.concatenate([src_cols, src_cols[:, :BODY]], axis=1),
        "dst_cols": dst_all.reshape(-1, P).T,
        "dst_groups": dst_all.reshape(-1, GROUP),
        "w1": np.asarray(L0_gnn_W1), "b1": np.asarray(L0_gnn_b1).reshape(1, D),
        "w2": np.asarray(L0_gnn_W2), "b2": np.asarray(L0_gnn_b2).reshape(1, D),
        "wl": np.asarray(L1_gnn_W_l).T, "bl": np.asarray(L1_gnn_b_l).reshape(1, D),
        "wr": np.asarray(L1_gnn_W_r).T,
    }
    arrays = {k: np.ascontiguousarray(v) for k, v in arrays.items()}
    nc = bacc.Bacc("TRN2", target_bir_lowering=False, num_devices=1)
    args = [nc.dram_tensor(k, v.shape, mybir.dt.from_np(v.dtype), kind="ExternalInput").ap() for k, v in arrays.items()]
    out = nc.dram_tensor("y_rows", (tiles * P, D), mybir.dt.float32, kind="ExternalOutput").ap()
    gnn_program(nc, n_nodes, *args, out)
    result = run_bass_kernel_spmd(nc, [arrays], core_ids=[0])
    return result.results[0]["y_rows"][:n_nodes]
```

```python
from contextlib import ExitStack

import concourse.bass as bass
from concourse import mybir

P = 128
D = 512
KD = D // P
CHUNKS = 4
GROUP = CHUNKS * P
SLOTS = 8
BODY = SLOTS * CHUNKS
SPLIT = 4
STAGE = 8
NEXTS = 2
COUNT = 16
LAG = 4
PE_LAG = 2
SUMS = 4
MINE = 4
RES = 4
EPS = 1e-5
SELF_LOOP_W = 2.0


def gnn_program(nc, n_nodes, x, src, dst, dst_groups, w1, b1, w2, b2, wl, bl, wr, out):
    fp32 = mybir.dt.float32
    fp32r = mybir.dt.float32r
    bf16 = mybir.dt.bfloat16
    i32 = mybir.dt.int32
    ALU = mybir.AluOpType
    ACT = mybir.ActivationFunctionType
    AX = mybir.AxisListType

    TILES = -(-n_nodes // P)
    ROWS = TILES * P
    GROUPS = dst_groups.shape[0]
    BODIES = GROUPS // SLOTS
    COLS = GROUPS * CHUNKS
    HALVES = -(-GROUPS // P)
    GROWS = GROUPS // HALVES
    LAST = TILES - 1
    assert n_nodes % P and GROUPS > SLOTS
    assert GROWS * HALVES == GROUPS and BODIES * SLOTS == GROUPS and TILES >= 6

    table = [nc.dram_tensor(f"table{n}", (ROWS, D), fp32, kind="Internal").ap() for n in range(3)]
    raw_dram = nc.dram_tensor("raw_ranges", (2, GROUPS), i32, kind="Internal").ap()
    range_dram = nc.dram_tensor("ranges_dram", (1, 2 * GROUPS + 1), i32, kind="Internal").ap()

    ctx = ExitStack()
    with ctx:
        def sb(name, shape, dt):
            return ctx.enter_context(nc.sbuf_tensor(name, shape, dt))

        def pb(name, shape, dt=fp32):
            return ctx.enter_context(nc.psum_tensor(name, shape, dt))

        def sem(name):
            return ctx.enter_context(nc.semaphore(name))

        mine = sb("mine", [P, MINE, D], fp32)
        stage = sb("stage", [P, STAGE, D], fp32)
        rows = sb("rows", [P, SLOTS, CHUNKS * D], fp32)
        part_hi = sb("part_hi", [P, SPLIT, CHUNKS * D], fp32r)
        part_lo = sb("part_lo", [P, SPLIT, CHUNKS * D], fp32r)
        onehot = sb("onehot", [P, SPLIT, CHUNKS, P], fp32r)
        onehot_next = sb("onehot_next", [P, NEXTS, CHUNKS, P], fp32r)
        weight_a = sb("weight_a", [P, KD, D], fp32)
        weight_b = sb("weight_b", [P, KD, D], fp32)
        bias = sb("bias", [P, D], fp32)
        ones = sb("ones", [1, P], fp32)
        agg_sb = sb("agg_sb", [P, D], fp32)
        aggT = sb("aggT", [P, D], fp32)
        pair = sb("pair", [P, 2, D], fp32)
        z = sb("z", [P, RES, D], fp32)
        dst_rel = sb("dst_rel", [P, COLS], fp32)
        src_slot = sb("src_slot", [P, SLOTS, CHUNKS], i32)
        window = sb("window", [P, 2 * P], bf16)
        ident = sb("ident", [P, P], fp32)
        twice = sb("twice", [P, P], fp32)
        zeros = sb("zeros", [P, P], bf16)
        span = sb("span", [P, 1], fp32)
        degree = sb("degree", [P, TILES], fp32)
        dinv = sb("dinv", [P, TILES], fp32)
        rmean = sb("rmean", [P, TILES], fp32)
        share = sb("share", [P, TILES], fp32)
        stats = sb("stats", [P, 6], fp32)
        moment = sb("moment", [P, 2], fp32)
        moments = sb("moments", [P, RES, 2], fp32)
        std = sb("std", [P, RES], fp32)
        rstd = sb("rstd", [P, RES], fp32)
        eps = sb("eps", [P, 1], fp32)
        mean_term = sb("mean_term", [P, RES], fp32)
        ranges = sb("ranges", [1, 2 * GROUPS + 2], i32)

        rows_flat = rows[:, :, :].rearrange("p s f -> p (s f)")
        at = [0]

        def early(width, dt, size=4):
            a = at[0]
            at[0] = a + -(-width * size // 4)
            v = rows_flat[:, a:at[0]]
            return v if dt == fp32 else v.bitcast(dt)

        dst_g = early(HALVES * GROUP, i32).rearrange("p (a e) -> p a e", a=HALVES)
        dst_c = early(COLS, i32)
        dst_bits = early(COLS, i32)
        node_in_tile = early(COLS, fp32)
        tile_of = early(COLS, fp32)
        node_hot = [early(COUNT * P, bf16, 2).rearrange("p (c n) -> p c n", c=COUNT) for _ in range(2)]
        tile_hot = [early(COUNT * TILES, bf16, 2).rearrange("p (c n) -> p c n", c=COUNT) for _ in range(2)]
        assert at[0] <= SLOTS * CHUNKS * D
        z_flat = z[:, :, :].rearrange("p a f -> p (a f)")
        raw_i = z_flat[0:1, 0:2 * GROUPS].bitcast(i32)
        raw_f = z_flat[0:1, 2 * GROUPS:4 * GROUPS]
        assert 4 * GROUPS <= RES * D
        group_range = pair[:, 0, 0:2 * HALVES].bitcast(i32).rearrange("p (m a) -> p m a", m=2)
        range_i = pair[:, 1, 0:2 * HALVES].bitcast(i32).rearrange("p (m a) -> p m a", m=2)
        masked_f = agg_sb[0:1, 0:2 * GROUPS + 1] if 2 * GROUPS + 1 <= D else None
        masked_i = aggT[0:1, 0:2 * GROUPS + 1].bitcast(i32)
        steps_f = bias[0:1, 0:GROUPS]
        steps_g = bias[0:1, GROUPS:2 * GROUPS]
        worst = rstd[0:1, 0:1]
        worst2 = rstd[0:1, 1:2]
        keep = rstd[0:1, 2:3]
        lo_all = agg_sb[:, 0:GROUPS + 1]
        lo_raw = aggT[:, 0:GROUPS + 1].bitcast(i32)

        agg_ps = pb("agg_ps", [P, SUMS, D])
        turn_ps = pb("turn_ps", [P, D])
        turn2_ps = pb("turn2_ps", [P, D])
        prod_ps = pb("prod_ps", [P, 2, D])
        count_ps = turn2_ps[:, 0:TILES]

        consts_made = sem("consts_made")
        edges_loaded = sem("edges_loaded")
        group_rows_loaded = sem("group_rows_loaded")
        raw_stored = sem("raw_stored")
        raw_loaded = sem("raw_loaded")
        raw_made = sem("raw_made")
        masked_made = sem("masked_made")
        masked_stored = sem("masked_stored")
        ranges_loaded = sem("ranges_loaded")
        lo_loaded = sem("lo_loaded")
        dve_chain = sem("dve_chain")
        passed = sem("passed")
        digits_made = sem("digits_made")
        node_hot_made = sem("node_hot_made")
        tile_hot_made = sem("tile_hot_made")
        hots_counted = sem("hots_counted")
        counted = sem("counted")
        degree_made = sem("degree_made")
        root_made = sem("root_made")
        x_loaded = [sem(f"x_loaded{n}") for n in range(8)]
        scaled = sem("scaled")
        rel_made = sem("rel_made")
        weights_loaded = [sem(f"weights_loaded{n}") for n in range(3)]
        own_weights_made = sem("own_weights_made")
        bias_loaded = [sem(f"bias_loaded{n}") for n in range(3)]
        stage_stored = sem("stage_stored")
        table_stored = [sem(f"table_stored{n}") for n in range(4)]
        src_loaded = [sem(f"src_loaded{s}") for s in range(SLOTS)]
        gathered = [sem(f"gathered{s}") for s in range(SLOTS)]
        hi_made = sem("hi_made")
        lo_made = sem("lo_made")
        onehot_made = sem("onehot_made")
        split_free = sem("split_free")
        agg_done = [sem(f"agg_done{n}") for n in range(3)]
        agg_taken = [sem(f"agg_taken{n}") for n in range(3)]
        own_taken = sem("own_taken")
        mine_loaded = [sem(f"mine_loaded{n}") for n in range(3)]
        onehot_next_made = sem("onehot_next_made")
        turned = [sem(f"turned{n}") for n in range(3)]
        aggT_made = [sem(f"aggT_made{n}") for n in range(3)]
        prod_done = [sem(f"prod_done{n}") for n in range(3)]
        prod_free = [sem(f"prod_free{n}") for n in range(3)]
        pair_loaded = sem("pair_loaded")
        std_made = [sem(f"std_made{n}") for n in range(3)]
        factors_made = [sem(f"factors_made{n}") for n in range(3)]
        stats_made = [sem(f"stats_made{n}") for n in range(3)]
        own_made = [sem(f"own_made{n}") for n in range(3)]

        tiles = []
        scale_of = [dinv, dinv, rmean]
        stored_to = [table[1], table[2], out]

        def passes_of(eng):
            return eng.value_load(ranges[0:1, 2 * GROUPS:2 * GROUPS + 1], min_val=1, max_val=TILES)

        def stand_alone(eng):
            eng.sem_inc(passed, 1)

        def as_tile(eng, value):
            tile = eng.alloc_register(f"tile{len(tiles)}")
            tiles.append(tile)
            eng.reg_mov(tile, value)
            return eng.snap(tile, min_val=0, max_val=LAST)

        def lo_of(eng, g, r):
            return as_tile(eng, eng.value_load(ranges[0:1, bass.ds(g, 1)], min_val=0, max_val=LAST) + r)

        def hi_of(eng, g, r):
            return as_tile(eng, eng.value_load(ranges[0:1, bass.ds(GROUPS + g, 1)], min_val=0, max_val=LAST) + r)

        def ahead(eng, t, k):
            return as_tile(eng, t + k)

        def back(eng, t, k):
            if isinstance(t, int):
                return t - k
            tile = eng.alloc_register(f"tile{len(tiles)}")
            tiles.append(tile)
            eng.reg_alu(tile, eng.snap(t - k), 0, ALU.max)
            return eng.snap(tile, min_val=0, max_val=LAST)

        in_rows = rows[:, :, :].rearrange("p s (c f) -> p (s c) f", f=D)
        used = -(-at[0] // D)
        pieces = []
        first = 0
        for size, place, after in ((STAGE, stage, "nothing"), (MINE, mine, "nothing"),
                                   (SLOTS * CHUNKS - used, in_rows[:, used:, :], "nothing"),
                                   (used, in_rows, "degrees"), (STAGE, stage, "stage")):
            last = min(first + size, TILES)
            for a in range(first, last, 9):
                b = min(a + 9, last)
                pieces.append((a, b, place[:, a - first:b - first, :], after))
            first = last
        assert len(pieces) <= 8 and last == TILES

        def load_piece(eng, n):
            a, b, place, _ = pieces[n]
            eng.dma_start(place, x[a * P:b * P, :].rearrange("(t p) f -> p t f", p=P)).then_inc(x_loaded[n], 16)

        block = ctx.enter_context(nc.Block())

        @block.sync
        def _(sp):
            sp.dma_start(dst_g[0:GROWS], dst_groups.rearrange("(a p) e -> p a e", p=GROWS)).then_inc(group_rows_loaded, 16)
            sp.dma_start(dst_c, dst).then_inc(edges_loaded, 16)
            for s in range(SLOTS):
                sp.dma_start(src_slot[:, s, :], src[:, s * CHUNKS:(s + 1) * CHUNKS]).then_inc(src_loaded[s], 16)
            sp.wait_ge(raw_made, 1)
            sp.dma_start(raw_dram.rearrange("m (a p) -> p m a", p=GROWS), range_i[0:GROWS],
                         allow_slow_non_contiguous=True).then_inc(raw_stored, 16)
            sp.wait_ge(raw_stored, 16)
            sp.dma_start(raw_i, raw_dram.rearrange("m (o g) -> o (m g)", o=1)).then_inc(raw_loaded, 16)
            sp.wait_ge(masked_made, 1)
            sp.dma_start(range_dram, masked_i).then_inc(masked_stored, 16)
            sp.wait_ge(masked_stored, 16)
            sp.dma_start(ranges[0:1, 0:2 * GROUPS + 1], range_dram).then_inc(ranges_loaded, 16)
            sp.dma_start(lo_raw[:, 0:GROUPS], range_dram[0:1, 0:GROUPS].to_broadcast([P, GROUPS]))\
              .then_inc(lo_loaded, 16)
            sp.dma_start(lo_raw[:, GROUPS:GROUPS + 1], range_dram[0:1, 2 * GROUPS:2 * GROUPS + 1].to_broadcast([P, 1]))\
              .then_inc(lo_loaded, 16)
            for n, (_, _, _, after) in enumerate(pieces):
                if after == "nothing":
                    load_piece(sp, n)
            sp.dma_start(weight_a[:, :, :], w1.rearrange("(k p) n -> p k n", p=P)).then_inc(weights_loaded[0], 16)
            sp.dma_start(weight_b[:, :, :], w2.rearrange("(k p) n -> p k n", p=P)).then_inc(weights_loaded[1], 16)
            sp.wait_ge(counted, 1)
            sp.wait_ge(rel_made, 1)
            sp.dma_start(bias[0:1, :], b1).then_inc(bias_loaded[0], 16)
            for n, (_, _, _, after) in enumerate(pieces):
                if after == "degrees":
                    load_piece(sp, n)
            for n, (_, _, _, after) in enumerate(pieces):
                if after == "stage":
                    sp.wait_ge(stage_stored, 16)
                    load_piece(sp, n)
            sp.wait_ge(ranges_loaded, 16)
            passes = passes_of(sp)
            for layer in range(3):
                if layer == 1:
                    sp.wait_ge(prod_done[0], TILES)
                    sp.dma_start(bias[0:1, :], b2).then_inc(bias_loaded[1], 16)
                    sp.dma_start(weight_a[:, :, :], wl.rearrange("(k p) n -> p k n", p=P))\
                      .then_inc(weights_loaded[2], 16)
                if layer == 2:
                    sp.wait_ge(prod_done[1], TILES)
                    sp.dma_start(bias[:, :], bl.to_broadcast([P, D])).then_inc(bias_loaded[2], 16)
                    sp.dma_start(weight_b[:, :, :], wr.rearrange("(k p) n -> p k n", p=P))\
                      .then_inc(weights_loaded[2], 16)
                base = sp.snap(passes * (layer * BODIES))
                with sp.Fori(0, passes) as r:
                    with sp.Fori(0, BODIES) as i:
                        n = sp.snap(base + r * BODIES + i + 1)
                        for s in range(SLOTS):
                            sp.wait_ge(gathered[s], n * (16 * CHUNKS))
                            sp.dma_start(src_slot[:, s, :], src[:, bass.ds(i * BODY + BODY + s * CHUNKS, CHUNKS)])\
                              .then_inc(src_loaded[s], 16)
            for s in range(SLOTS):
                sp.wait_ge(src_loaded[s], sp.snap(passes * (3 * BODIES * 16) + 16))
            stand_alone(sp)

        @block.gpsimd
        def _(pool):
            pool.iota(window[:, :], pattern=[[1, 2 * P]], base=0, channel_multiplier=0,
                      allow_small_or_imprecise_dtypes=True).then_inc(consts_made, 1)
            pool.memset(zeros[:, :], 0.0).then_inc(consts_made, 1)
            pool.memset(eps[:, :], EPS).then_inc(consts_made, 1)
            pool.memset(ones[:, :], 1.0).then_inc(consts_made, 1)
            pool.memset(ident[:, :], 0.0).then_inc(consts_made, 1)
            pool.memset(twice[:, :], 0.0).then_inc(consts_made, 1)
            pool.wait_ge(consts_made, 6)
            for m, v in ((ident, 1.0), (twice, SELF_LOOP_W)):
                pool.affine_select(out=m[:, :], in_=m[:, :], compare_op=ALU.not_equal, fill=v, base=0,
                                   pattern=[[-1, P]], channel_multiplier=1).then_inc(consts_made, 1)
            pool.wait_ge(ranges_loaded, 16)
            passes = passes_of(pool)
            for layer in range(3):
                if layer == 0:
                    pool.wait_ge(stage_stored, 16)
                pool.wait_ge(table_stored[layer], 16 * (len(pieces) - 1 if layer == 0 else TILES + RES))
                base = pool.snap(passes * (layer * BODIES))
                with pool.Fori(0, passes) as r:
                    with pool.Fori(0, BODIES) as i:
                        n = pool.snap(base + r * BODIES + i)
                        for s in range(SLOTS):
                            pool.wait_ge(src_loaded[s], n * 16 + 16)
                            pool.wait_ge(lo_made, n * SLOTS + (s + 1))
                            stand_alone(pool)
                            for c in range(CHUNKS):
                                pool.indirect_dma_start(
                                    rows[:, s, c * D:(c + 1) * D], None, table[layer],
                                    bass.IndirectOffsetOnAxis(ap=src_slot[:, s, c:c + 1], axis=0))\
                                    .then_inc(gathered[s], 16)

        @block.scalar
        def _(act):
            act.wait_ge(consts_made, 8)
            act.wait_ge(degree_made, 1)
            act.activation(degree[:, :], degree[:, :], ACT.Sqrt).then_inc(root_made, 1)
            for n, (a, b, place, _) in enumerate(pieces):
                act.wait_ge(scaled, n + 1)
                act.dma_start(table[0][a * P:b * P, :].rearrange("(t p) f -> p t f", p=P), place)\
                   .then_inc(stage_stored if n == 0 else table_stored[0], 16)
            act.wait_ge(ranges_loaded, 16)
            passes = passes_of(act)
            seen = act.alloc_register("act_seen")
            for layer in range(3):
                normed = layer > 0

                def take_sums(t):
                    act.wait_ge(turned[layer], t + 1)
                    if layer == 2:
                        act.wait_ge(mine_loaded[layer], t * 16 + 16)
                        act.activation(pair[:, 0, :], mine[:, bass.ds(t % MINE, 1), :], ACT.Copy).then_inc(own_taken, 1)
                    act.wait_ge(agg_done[layer], t + 1)
                    act.activation(agg_sb[:, :], agg_ps[:, bass.ds(t % SUMS, 1), :], ACT.Identity,
                                   scale=scale_of[layer][:, bass.ds(t, 1)]).then_inc(agg_taken[layer], 1)

                def take_turned(k):
                    act.wait_ge(turned[layer], k + 2)
                    if layer == 2:
                        act.activation(pair[:, 1, :], turn2_ps[:, :], ACT.Copy)
                    act.activation(aggT[:, :], turn_ps[:, :], ACT.Copy).then_inc(aggT_made[layer], 1)

                def relu_first(k):
                    act.wait_ge(prod_done[layer], k + 1)
                    act.wait_ge(table_stored[layer + 1], k * 16 + 16)
                    act.activation(z[:, bass.ds(k % RES, 1), :], prod_ps[:, bass.ds(k % 2, 1), :], ACT.Relu,
                                   scale=dinv[:, bass.ds(k, 1)]).then_inc(prod_free[layer], 1)

                def take_root(k):
                    act.wait_ge(stats_made[layer], k + 1)
                    slot = bass.ds(k % RES, 1)
                    act.activation(std[:, slot], moments[:, slot, 1:2], ACT.Sqrt,
                                   bias=eps[:, 0:1]).then_inc(std_made[layer], 1)

                def normalise(k):
                    act.wait_ge(factors_made[layer], k + 1)
                    zk = z[:, bass.ds(k % RES, 1), :]
                    act.activation(zk, zk, ACT.Identity, bias=mean_term[:, bass.ds(k % RES, 1)],
                                   scale=rstd[:, bass.ds(k % RES, 1)]).then_inc(own_made[layer], 1)

                def load_x(k):
                    act.wait_ge(prod_free[layer], k + 1)
                    act.dma_start(pair[:, bass.ds(k % 2, 1), :], x[bass.ds(k * P, P), :]).then_inc(pair_loaded, 16)

                def load_mine(k):
                    act.wait_ge(mine_loaded[layer], k * 16)
                    if layer == 2:
                        act.wait_ge(own_taken, k + 1)
                    act.dma_start(mine[:, bass.ds(k % MINE, 1), :], table[layer][bass.ds(k * P, P), :])\
                       .then_inc(mine_loaded[layer], 16)

                def store(k):
                    if normed:
                        act.wait_ge(own_made[layer], k + 1)
                    else:
                        act.wait_ge(prod_free[layer], k + 3)
                    act.wait_ge(table_stored[layer + 1], k * 16 + 16 * RES)
                    act.dma_start(stored_to[layer][bass.ds(k * P, P), :], z[:, bass.ds(k % RES, 1), :])\
                       .then_inc(table_stored[layer + 1], 16)

                def step(t):
                    with act.If(t > 0):
                        take_turned(back(act, t, 1))
                    act.nop()
                    take_sums(t)
                    if normed:
                        with act.If(t > 2):
                            take_root(back(act, t, 3))
                        act.nop()
                    with act.If(t < LAST - 1):
                        load_mine(ahead(act, t, 2))
                    act.nop()
                    if layer == 1:
                        with act.If(t > 1):
                            k = back(act, t, 1)
                            act.wait_ge(pair_loaded, k * 16)
                            load_x(k)
                        act.nop()
                    if normed:
                        with act.If(t > 4):
                            store(back(act, t, 5))
                        act.nop()
                        with act.If(t > 3):
                            normalise(back(act, t, 4))
                        act.nop()
                    else:
                        with act.If(t > 2):
                            store(back(act, t, 3))
                        act.nop()
                        with act.If(t > 1):
                            relu_first(back(act, t, 2))
                        act.nop()

                if layer == 1:
                    act.dma_start(pair[:, 0, :], x[0:P, :]).then_inc(pair_loaded, 16)
                if layer == 0:
                    act.wait_ge(stage_stored, 16)
                act.wait_ge(table_stored[layer], 16 * (len(pieces) - 1 if layer == 0 else TILES + RES))
                act.dma_start(mine[:, 0, :], table[layer][0:P, :]).then_inc(mine_loaded[layer], 16)
                act.wait_ge(mine_loaded[layer], 16)
                act.dma_start(mine[:, 1, :], table[layer][P:2 * P, :]).then_inc(mine_loaded[layer], 16)
                act.reg_mov(seen, 0)
                base = act.snap(passes * (layer * BODIES * SLOTS))
                before = [act.alloc_register(f"act_before{layer}_{s}") for s in range(LAG)]
                for s in range(LAG):
                    act.reg_mov(before[s], 0)
                with act.Fori(0, passes) as r:
                    with act.Fori(0, BODIES) as i:
                        n = act.snap(base + (r * BODIES + i) * SLOTS)
                        m = act.snap((passes * (layer * BODIES) + r * BODIES + i + 1) * (16 * CHUNKS))
                        for s in range(SLOTS):
                            act.wait_ge(split_free, n + (s + 1))
                            act.wait_ge(gathered[s], m)
                            act.activation(part_hi[:, s % SPLIT, :], rows[:, s, :], ACT.Copy).then_inc(hi_made, 1)
                            done = act.snap(before[s % LAG], min_val=0, max_val=LAST)
                            first = act.snap(seen, min_val=0, max_val=LAST)
                            with act.If(done > first):
                                with act.Fori(first, done) as t:
                                    step(as_tile(act, t))
                                act.reg_mov(seen, done)
                            act.reg_mov(before[s % LAG], hi_of(act, i * SLOTS + s, r))
                first = act.snap(seen, min_val=0, max_val=LAST)
                with act.If(first < LAST):
                    with act.Fori(first, LAST) as t:
                        step(as_tile(act, t))
                act.nop()
                t = LAST
                take_turned(t - 1)
                take_sums(t)
                if normed:
                    take_root(t - 3)
                if layer == 1:
                    act.wait_ge(pair_loaded, 16 * (t - 1))
                    load_x(back(act, t, 1))
                    act.wait_ge(pair_loaded, 16 * t)
                    load_x(t)
                if normed:
                    store(back(act, t, 5))
                    normalise(back(act, t, 4))
                    take_turned(t)
                    for k in range(t - 2, t + 1):
                        take_root(k)
                        store(k - 2)
                        normalise(k - 1)
                    store(t - 1)
                    normalise(t)
                    store(t)
                else:
                    store(t - 3)
                    relu_first(t - 2)
                    take_turned(t)
                    for k in range(t - 1, t + 1):
                        store(k - 1)
                        relu_first(k)
                    store(t)
            act.wait_ge(table_stored[3], 16 * (TILES + RES))

        @block.vector
        def _(dve):
            chain = [0]

            def link(ins):
                chain[0] += 1
                ins.then_inc(dve_chain, 1)
                dve.wait_ge(dve_chain, chain[0])

            dve.wait_ge(group_rows_loaded, 16)
            link(dve.tensor_reduce(group_range[0:GROWS, 0, :], dst_g[0:GROWS], AX.X, ALU.min))
            link(dve.tensor_reduce(group_range[0:GROWS, 1, :], dst_g[0:GROWS], AX.X, ALU.max))
            dve.tensor_scalar(range_i[0:GROWS], group_range[0:GROWS], 7, None, ALU.arith_shift_right)\
               .then_inc(raw_made, 1)
            dve.wait_ge(edges_loaded, 16)
            link(dve.tensor_scalar(dst_bits, dst_c, P - 1, None, ALU.bitwise_and))
            link(dve.tensor_copy(node_in_tile, dst_bits))
            link(dve.tensor_scalar(dst_bits, dst_c, 7, None, ALU.arith_shift_right))
            dve.tensor_copy(tile_of, dst_bits).then_inc(digits_made, 1)
            dve.tensor_copy(dst_rel[:, :], dst_c).then_inc(digits_made, 1)
            dve.wait_ge(consts_made, 8)
            dve.wait_ge(digits_made, 2)
            with dve.Fori(0, COLS // (2 * COUNT)) as i:
                for s in range(2):
                    dve.wait_ge(hots_counted, i * 2 + (s + 1))
                    for c in range(COUNT):
                        made = dve.tensor_scalar(node_hot[s][:, c, :], window[:, 0:P],
                                                 node_in_tile[:, bass.ds((i * 2 + s) * COUNT + c, 1)], None, ALU.is_equal)
                    made.then_inc(node_hot_made, 1)
                    dve.tensor_tensor(
                        tile_hot[s][:, :, :],
                        window[:, 0:TILES].rearrange("p (o n) -> p o n", o=1).to_broadcast([P, COUNT, TILES]),
                        tile_of[:, bass.ds((i * 2 + s) * COUNT, COUNT)].rearrange("p (c o) -> p c o", o=1)
                        .to_broadcast([P, COUNT, TILES]),
                        ALU.is_equal).then_inc(tile_hot_made, 1)
            dve.wait_ge(raw_loaded, 16)
            link(dve.tensor_copy(raw_f, raw_i))
            lo_f, hi_f = raw_f[:, 0:GROUPS], raw_f[:, GROUPS:2 * GROUPS]
            link(dve.tensor_tensor(steps_f, hi_f, lo_f, ALU.subtract))
            link(dve.tensor_reduce(worst, steps_f, AX.X, ALU.max))
            link(dve.tensor_tensor(steps_g[:, 0:GROUPS - 1], hi_f[:, 0:GROUPS - 1], lo_f[:, 1:GROUPS], ALU.subtract))
            link(dve.tensor_reduce(worst2, steps_g[:, 0:GROUPS - 1], AX.X, ALU.max))
            link(dve.tensor_scalar(worst, worst, 1.0, None, ALU.subtract))
            link(dve.tensor_tensor(worst, worst, worst2, ALU.max))
            link(dve.tensor_reduce(worst2, steps_g[:, 0:GROUPS - 1], AX.X, ALU.min))
            link(dve.tensor_scalar(worst2, worst2, -1.0, -1.0, ALU.mult, ALU.add))
            link(dve.tensor_tensor(worst, worst, worst2, ALU.max))
            reach = LAG + 1
            link(dve.tensor_tensor(steps_f[:, 0:GROUPS - reach], hi_f[:, reach:GROUPS], hi_f[:, 0:GROUPS - reach],
                                   ALU.subtract))
            link(dve.tensor_reduce(worst2, steps_f[:, 0:GROUPS - reach], AX.X, ALU.max))
            link(dve.tensor_tensor(worst2, worst2, hi_f[:, reach - 1:reach], ALU.max))
            link(dve.tensor_scalar(worst2, worst2, 3.0, None, ALU.subtract))
            link(dve.tensor_tensor(worst, worst, worst2, ALU.max))
            link(dve.tensor_tensor(worst, worst, lo_f[:, 0:1], ALU.max))
            link(dve.tensor_scalar(keep, worst, 1.0, None, ALU.is_lt))
            link(dve.tensor_scalar(masked_f[:, 0:2 * GROUPS], raw_f, keep, None, ALU.mult))
            link(dve.tensor_scalar(masked_f[:, 2 * GROUPS:2 * GROUPS + 1], keep, -float(TILES - 1), float(TILES),
                                   ALU.mult, ALU.add))
            dve.tensor_copy(masked_i, masked_f).then_inc(masked_made, 1)
            dve.wait_ge(counted, 1)
            link(dve.tensor_copy(rmean[:, :], count_ps))
            dve.tensor_scalar(degree[:, :], rmean[:, :], SELF_LOOP_W, None, ALU.add).then_inc(degree_made, 1)
            link(dve.tensor_scalar(dinv[:, :], rmean[:, :], 1.0, None, ALU.max))
            link(dve.tensor_copy(share[:, :], rmean[:, :]))
            link(dve.reciprocal(rmean[:, :], dinv[:, :]))
            link(dve.tensor_tensor(share[:, :], share[:, :], rmean[:, :], ALU.mult))
            dve.wait_ge(root_made, 1)
            link(dve.reciprocal(dinv[:, :], degree[:, :]))
            dve.wait_ge(lo_loaded, 32)
            link(dve.tensor_copy(lo_all, lo_raw))
            link(dve.tensor_scalar(lo_all, lo_all, float(P), None, ALU.mult))
            rel = dst_rel[:, :].rearrange("p (g c) -> p g c", c=CHUNKS)
            link(dve.tensor_tensor(rel, rel, lo_all[:, 0:GROUPS].rearrange("p (g o) -> p g o", o=1)
                                   .to_broadcast([P, GROUPS, CHUNKS]), ALU.subtract))
            dve.sem_inc(rel_made, 1)
            dve.tensor_copy(span[:, :], lo_all[:, GROUPS:GROUPS + 1])
            for n, (a, b, place, _) in enumerate(pieces):
                dve.wait_ge(x_loaded[n], 16)
                for t in range(a, b):
                    last = dve.tensor_scalar(place[:, t - a, :], place[:, t - a, :], dinv[:, t:t + 1], None, ALU.mult)
                last.then_inc(scaled, 1)
            dve.wait_ge(ranges_loaded, 16)
            passes = passes_of(dve)
            seen = dve.alloc_register("dve_seen")
            links = dve.alloc_register("dve_links")
            linked = sem("linked")
            dve.reg_mov(links, 0)
            next_used = [dve.alloc_register(f"dve_next_used{q}") for q in range(NEXTS)]
            for q in range(NEXTS):
                dve.reg_mov(next_used[q], SPLIT)
            for layer in range(3):
                def marked(ins):
                    ins.then_inc(linked, 1)
                    v = dve.snap(dve.snap(links) + 1)
                    dve.reg_mov(links, v)
                    return v

                def until(v):
                    dve.wait_ge(linked, v)
                    stand_alone(dve)

                def chained(ins):
                    until(marked(ins))

                def take_stats(k, f=None):
                    dve.wait_ge(prod_done[layer], k + 1)
                    dve.wait_ge(table_stored[layer + 1], k * 16 + 16)
                    slot = bass.ds(k % RES, 1)
                    zk = z[:, slot, :]
                    pk = prod_ps[:, bass.ds(k % 2, 1), :]
                    if layer == 1:
                        dve.wait_ge(pair_loaded, k * 16 + 16)
                        ins = dve.scalar_tensor_tensor(out=zk, in0=pk, scalar=0.0, in1=pair[:, bass.ds(k % 2, 1), :],
                                                       op0=ALU.max, op1=ALU.add)
                    else:
                        ins = dve.scalar_tensor_tensor(out=zk, in0=bias[:, :].rearrange("p (o f) -> p o f", o=1),
                                                       scalar=share[:, bass.ds(k, 1)], in1=pk,
                                                       op0=ALU.mult, op1=ALU.add)
                    ins.then_inc(prod_free[layer], 1)
                    if f is not None:
                        made = make_reciprocal(f)
                    dve.wait_ge(prod_free[layer], k + 3)
                    stand_alone(dve)
                    taken = marked(dve.bn_stats(stats[:, :], zk))
                    if f is not None:
                        make_mean_term(f, made)
                    until(taken)
                    until(marked(dve.bn_aggr(moment[:, :], stats[:, :])))
                    dve.tensor_copy(moments[:, slot, :], moment[:, :]).then_inc(stats_made[layer], 1)

                def make_reciprocal(f):
                    dve.wait_ge(std_made[layer], f + 1)
                    slot = bass.ds(f % RES, 1)
                    return marked(dve.reciprocal(rstd[:, slot], std[:, slot]))

                def make_mean_term(f, made):
                    slot = bass.ds(f % RES, 1)
                    until(made)
                    dve.scalar_tensor_tensor(out=mean_term[:, slot], in0=moments[:, slot, 0:1], scalar=-1.0,
                                             in1=rstd[:, slot].rearrange("p (o m) -> p o m", o=1),
                                             op0=ALU.mult, op1=ALU.mult).then_inc(factors_made[layer], 1)

                def make_factors(f):
                    make_mean_term(f, make_reciprocal(f))

                def step(t):
                    with dve.If(t > 2):
                        take_stats(back(dve, t, 2), back(dve, t, 3))
                    with dve.Else():
                        with dve.If(t > 1):
                            take_stats(back(dve, t, 2))
                        dve.nop()

                if layer == 2:
                    dve.wait_ge(weights_loaded[2], 32)
                    for j in range(KD):
                        block_j = weight_b[:, j, j * P:(j + 1) * P]
                        dve.tensor_tensor(block_j, block_j, ident[:, :], ALU.add).then_inc(own_weights_made, 1)
                    dve.wait_ge(bias_loaded[2], 16)
                dve.reg_mov(seen, 0)
                before = [dve.alloc_register(f"dve_before{layer}_{s}") for s in range(LAG)]
                for s in range(LAG):
                    dve.reg_mov(before[s], 0)
                base = dve.snap(passes * (layer * BODIES * SLOTS))
                with dve.Fori(0, passes) as r:
                    with dve.Fori(0, BODIES) as i:
                        n = dve.snap(base + (r * BODIES + i) * SLOTS)
                        for s in range(SLOTS):
                            dve.wait_ge(split_free, n + (s + 1))
                            for c in range(CHUNKS):
                                made = dve.tensor_scalar(onehot[:, s % SPLIT, c, :], window[:, 0:P],
                                                         dst_rel[:, bass.ds(i * BODY + (s * CHUNKS + c), 1)], None,
                                                         ALU.is_equal)
                            made.then_inc(onehot_made, 1)
                            dve.wait_ge(hi_made, n + (s + 1))
                            dve.tensor_tensor(part_lo[:, s % SPLIT, :], rows[:, s, :], part_hi[:, s % SPLIT, :],
                                              ALU.subtract).then_inc(lo_made, 1)
                            lo = lo_of(dve, i * SLOTS + s, r)
                            hi = hi_of(dve, i * SLOTS + s, r)
                            with dve.If(hi > lo):
                                dve.wait_ge(split_free, dve.snap(next_used[s % NEXTS]))
                                for c in range(CHUNKS):
                                    made = dve.tensor_scalar(onehot_next[:, s % NEXTS, c, :], window[:, P:2 * P],
                                                             dst_rel[:, bass.ds(i * BODY + (s * CHUNKS + c), 1)], None,
                                                             ALU.is_equal)
                                made.then_inc(onehot_next_made, 1)
                                dve.reg_mov(next_used[s % NEXTS], dve.snap(n + (s + 1 + SPLIT)))
                            if layer == 0:
                                continue
                            done = dve.snap(before[s % LAG], min_val=0, max_val=LAST)
                            first = dve.snap(seen, min_val=0, max_val=LAST)
                            with dve.If(done > first):
                                with dve.Fori(first, done) as t:
                                    step(as_tile(dve, t))
                                dve.reg_mov(seen, done)
                            dve.reg_mov(before[s % LAG], hi)
                    dve.wait_ge(onehot_made, dve.snap(base + r * GROUPS + GROUPS))
                    chained(dve.tensor_scalar(dst_rel[:, :], dst_rel[:, :], float(P), None, ALU.subtract))
                chained(dve.tensor_scalar(dst_rel[:, :], dst_rel[:, :], span[:, :], None, ALU.add))
                if layer == 0:
                    continue
                first = dve.snap(seen, min_val=0, max_val=LAST)
                with dve.If(first < LAST):
                    with dve.Fori(first, LAST) as t:
                        step(as_tile(dve, t))
                dve.nop()
                for k in range(LAST - 2, LAST + 1):
                    take_stats(k, k - 1)
                make_factors(LAST)

        @block.tensor
        def _(pe):
            pe.wait_ge(consts_made, 8)
            wide_zeros = zeros[:, :].rearrange("p (o n) -> p o n", o=1).to_broadcast([P, KD, P])

            pe.sem_inc(hots_counted, 2)
            pe.sem_inc(lo_made, SLOTS)
            pe.sem_inc(split_free, SPLIT)
            pe.sem_inc(own_taken, MINE)
            for layer in range(3):
                pe.sem_inc(turned[layer], 1)
                pe.sem_inc(agg_taken[layer], SUMS - 1)
                pe.sem_inc(prod_free[layer], 2)
                pe.sem_inc(table_stored[layer + 1], 16 * RES)
            pe.matmul(count_ps, zeros[:, :], zeros[:, 0:TILES], start=True, stop=False)
            with pe.Fori(0, COLS // (2 * COUNT)) as i:
                for s in range(2):
                    pe.wait_ge(node_hot_made, i * 2 + (s + 1))
                    pe.wait_ge(tile_hot_made, i * 2 + (s + 1))
                    for c in range(COUNT):
                        last = pe.matmul(count_ps, node_hot[s][:, c, :], tile_hot[s][:, c, :], start=False, stop=False)
                    last.then_inc(hots_counted, 1)
            pe.matmul(count_ps, zeros[:, :], zeros[:, 0:TILES], start=False, stop=True).then_inc(counted, 1)

            pe.wait_ge(ranges_loaded, 16)
            passes = passes_of(pe)
            cur = pe.alloc_register("pe_cur")
            seen = pe.alloc_register("pe_seen")
            met_two = pe.alloc_register("pe_met_two")
            pe.reg_mov(met_two, 0)
            for layer in range(3):
                weight = [weight_a, weight_b, weight_a][layer]

                def multiply(k):
                    pe.wait_ge(aggT_made[layer], k + 1)
                    pe.wait_ge(prod_free[layer], k + 1)
                    to = prod_ps[:, bass.ds(k % 2, 1), :]
                    if layer < 2:
                        pe.matmul(to, ones[:, :], bias[0:1, :], start=True, stop=False)
                    for j in range(KD):
                        last = pe.matmul(to, aggT[:, j * P:(j + 1) * P], weight[:, j, :], start=(layer == 2 and j == 0),
                                         stop=(layer < 2 and j == KD - 1))
                    if layer == 2:
                        for j in range(KD):
                            last = pe.matmul(to, pair[:, 1, j * P:(j + 1) * P], weight_b[:, j, :], start=False,
                                             stop=(j == KD - 1))
                    last.then_inc(prod_done[layer], 1)

                def turn(k):
                    pe.wait_ge(agg_taken[layer], k + SUMS)
                    if layer == 2:
                        pe.wait_ge(own_taken, k + (1 + MINE))
                        for j in range(KD):
                            pe.transpose(turn2_ps[:, j * P:(j + 1) * P], pair[:, 0, j * P:(j + 1) * P], ident[:, :])
                    for j in range(KD):
                        last = pe.transpose(turn_ps[:, j * P:(j + 1) * P], agg_sb[:, j * P:(j + 1) * P], ident[:, :])
                    last.then_inc(turned[layer], 1)

                def close(t):
                    to = agg_ps[:, bass.ds(t % SUMS, 1), :]
                    if layer < 2:
                        pe.wait_ge(mine_loaded[layer], t * 16 + 16)
                        last = pe.matmul(to, twice[:, :], mine[:, bass.ds(t % MINE, 1), :], start=False, stop=True)
                    else:
                        last = pe.matmul(to, zeros[:, :], wide_zeros, start=False, stop=True)
                    last.then_inc(agg_done[layer], 1)

                def open_next(t):
                    if not isinstance(t, int):
                        pe.wait_ge(agg_taken[layer], t + 1)
                    bank = (t + 1) % SUMS
                    pe.matmul(agg_ps[:, bass.ds(bank, 1), :], zeros[:, :], wide_zeros, start=True, stop=False)

                def finish(t):
                    close(t)
                    open_next(t)

                def step(t):
                    with pe.If(t > 0):
                        multiply(back(pe, t, 1))
                    pe.nop()
                    turn(t)

                def add_chunks(t, q, hots, chunks):
                    to = agg_ps[:, bass.ds(t % SUMS, 1), :]
                    for c in chunks:
                        hot = hots[:, c, :]
                        pe.matmul(to, hot, part_hi[:, q, c * D:(c + 1) * D], start=False, stop=False)
                        last = pe.matmul(to, hot, part_lo[:, q, c * D:(c + 1) * D], start=False, stop=False)
                    return last

                if layer < 2:
                    pe.wait_ge(weights_loaded[layer], 16)
                    pe.wait_ge(bias_loaded[layer], 16)
                else:
                    pe.wait_ge(own_weights_made, KD)
                open_next(-1)
                pe.reg_mov(cur, 0)
                pe.reg_mov(seen, 0)
                before = [pe.alloc_register(f"pe_before{layer}_{s}") for s in range(PE_LAG)]
                for s in range(PE_LAG):
                    pe.reg_mov(before[s], 0)
                base = pe.snap(passes * (layer * BODIES * SLOTS))
                with pe.Fori(0, passes) as r:
                    with pe.Fori(0, BODIES) as i:
                        n = pe.snap(base + (r * BODIES + i) * SLOTS)
                        for s in range(SLOTS):
                            lo = lo_of(pe, i * SLOTS + s, r)
                            hi = hi_of(pe, i * SLOTS + s, r)
                            first = pe.snap(cur, min_val=0, max_val=LAST)
                            with pe.If(lo > first):
                                with pe.Fori(first, lo) as t:
                                    finish(as_tile(pe, t))
                            pe.nop()
                            pe.wait_ge(onehot_made, n + (s + 1))
                            pe.wait_ge(hi_made, n + (s + 1))
                            pe.wait_ge(lo_made, n + (s + 1 + SLOTS))
                            add_chunks(lo, s % SPLIT, onehot[:, s % SPLIT], range(CHUNKS - 1))
                            with pe.If(hi > lo):
                                add_chunks(lo, s % SPLIT, onehot[:, s % SPLIT], range(CHUNKS - 1, CHUNKS))
                                finish(lo)
                                v = pe.snap(pe.snap(met_two) + 1)
                                pe.reg_mov(met_two, v)
                                pe.wait_ge(onehot_next_made, v)
                                last = add_chunks(hi, s % SPLIT, onehot_next[:, s % NEXTS], range(CHUNKS))
                                last.then_inc(split_free, 1)
                            with pe.Else():
                                add_chunks(lo, s % SPLIT, onehot[:, s % SPLIT], range(CHUNKS - 1, CHUNKS)).then_inc(split_free, 1)
                            pe.reg_mov(cur, hi)
                            done = pe.snap(before[s % PE_LAG], min_val=0, max_val=LAST)
                            first = pe.snap(seen, min_val=0, max_val=LAST)
                            with pe.If(done > first):
                                with pe.Fori(first, done) as t:
                                    step(as_tile(pe, t))
                                pe.reg_mov(seen, done)
                            pe.reg_mov(before[s % PE_LAG], hi)
                close(LAST)
                first = pe.snap(seen, min_val=0, max_val=LAST)
                with pe.If(first < LAST):
                    with pe.Fori(first, LAST) as t:
                        step(as_tile(pe, t))
                pe.nop()
                multiply(LAST - 1)
                turn(LAST)
                multiply(LAST)


def kernel(x, src, dst, L0_gnn_W1, L0_gnn_b1, L0_gnn_W2, L0_gnn_b2, L1_gnn_W_l, L1_gnn_b_l, L1_gnn_W_r):
    import numpy as np
    import concourse.bacc as bacc
    from concourse.bass_utils import run_bass_kernel_spmd

    x, src, dst = np.asarray(x), np.asarray(src), np.asarray(dst)
    n_nodes, n_edges = x.shape[0], src.shape[0]
    tiles = -(-n_nodes // P)
    bodies = -(-n_edges // (BODY * P))
    edges = bodies * BODY * P
    x_rows = np.zeros((tiles * P, D), x.dtype)
    x_rows[:n_nodes] = x
    src_all = np.zeros(edges, src.dtype)
    src_all[:n_edges] = src
    dst_all = np.full(edges, n_nodes, dst.dtype)
    dst_all[:n_edges] = dst
    src_cols = src_all.reshape(-1, P).T
    arrays = {
        "x_rows": x_rows,
        "src_cols": np.concatenate([src_cols, src_cols[:, :BODY]], axis=1),
        "dst_cols": dst_all.reshape(-1, P).T,
        "dst_groups": dst_all.reshape(-1, GROUP),
        "w1": np.asarray(L0_gnn_W1), "b1": np.asarray(L0_gnn_b1).reshape(1, D),
        "w2": np.asarray(L0_gnn_W2), "b2": np.asarray(L0_gnn_b2).reshape(1, D),
        "wl": np.asarray(L1_gnn_W_l).T, "bl": np.asarray(L1_gnn_b_l).reshape(1, D),
        "wr": np.asarray(L1_gnn_W_r).T,
    }
    arrays = {k: np.ascontiguousarray(v) for k, v in arrays.items()}
    nc = bacc.Bacc("TRN2", target_bir_lowering=False, num_devices=1)
    args = [nc.dram_tensor(k, v.shape, mybir.dt.from_np(v.dtype), kind="ExternalInput").ap() for k, v in arrays.items()]
    out = nc.dram_tensor("y_rows", (tiles * P, D), mybir.dt.float32, kind="ExternalOutput").ap()
    gnn_program(nc, n_nodes, *args, out)
    result = run_bass_kernel_spmd(nc, [arrays], core_ids=[0])
    return result.results[0]["y_rows"][:n_nodes]
```
